# Optimizing a Trainium2 kernel written in Bass

```python
import numpy as np
import jax
import jax.numpy as jnp

def _softmax(x, axis=-1):
    return jax.nn.softmax(x, axis=axis)

def _gelu(x):
    return jax.nn.gelu(x, approximate=True)

def _silu(x):
    return jax.nn.silu(x)

def _sigmoid(x):
    return jax.nn.sigmoid(x)

def _layernorm(x, axis=-1, eps=1e-05):
    m = jnp.mean(x, axis=axis, keepdims=True)
    v = jnp.var(x, axis=axis, keepdims=True)
    return (x - m) / jnp.sqrt(v + eps)

def _scatter_add(tgt, idx, src, axis=0):
    return tgt.at[idx].add(src)

def _segment_sum(src, seg, n):
    return jax.ops.segment_sum(src, seg, n)
kernel_name = 'mk_audio_tower_d1_tok_audfeat512_r4_236433'

def setup_inputs(seed: int=0):
    np.random.seed(seed)
    _w = jnp.asarray

    def _rec_inputs():
        import jax
        import jax.numpy as jnp
        _rk = jax.random.key(seed)
        x = -0.0003702 + 0.999946 * jax.random.normal(jax.random.fold_in(_rk, 1), (16, 64, 750), jnp.float32)
        return x
    x = _rec_inputs()

    def _L0_tok_setup():
        import jax, jax.numpy as jnp
        import numpy as np
        PATCH_SIZE = 200
        EMBED_DIM = 128
        IN_FEATURES = 2 * (PATCH_SIZE // 2 + 1)
        HIDDEN = 4 * IN_FEATURES
        key = jax.random.key(seed)
        k_x, k_w1, k_b1, k_w2, k_b2 = jax.random.split(key, 5)
        scale1 = 1.0 / np.sqrt(IN_FEATURES)
        scale2 = 1.0 / np.sqrt(HIDDEN)
        return {'x': jax.random.normal(k_x, (64, 64, 1000), dtype=jnp.float32), 'w1': jax.random.normal(k_w1, (IN_FEATURES, HIDDEN), dtype=jnp.float32) * scale1, 'b1': jax.random.normal(k_b1, (HIDDEN,), dtype=jnp.float32) * scale1, 'w2': jax.random.normal(k_w2, (HIDDEN, EMBED_DIM), dtype=jnp.float32) * scale2, 'b2': jax.random.normal(k_b2, (EMBED_DIM,), dtype=jnp.float32) * scale2}
    _L0_tok_all = _L0_tok_setup()
    _L0_tok_in = {k: v for k, v in _L0_tok_all.items() if k in ('w1', 'b1', 'w2', 'b2')}
    del _L0_tok_all

    def _L0_attn_setup():
        import jax, jax.numpy as jnp
        import numpy as np
        HEADS = 8
        DIM_HEAD = 64
        SCALE = DIM_HEAD ** (-0.5)
        DIM = 128
        INNER = HEADS * DIM_HEAD

        def sparsemax(z):
            n = z.shape[-1]
            z_sorted = jnp.flip(jnp.sort(z, axis=-1), axis=-1)
            cssv = jnp.cumsum(z_sorted, axis=-1)
            r = jnp.arange(1, n + 1, dtype=z.dtype)
            support = 1.0 + r * z_sorted > cssv
            k = jnp.sum(support, axis=-1, keepdims=True)
            tau = (jnp.take_along_axis(cssv, k - 1, axis=-1) - 1.0) / k.astype(z.dtype)
            return jnp.maximum(z - tau, 0.0)
        key = jax.random.key(seed)
        k1, k2, k3, k4 = jax.random.split(key, 4)
        B, N = (2, 512)
        x = jax.random.normal(k1, (B, N, DIM), dtype=jnp.float32)
        W_qkv = jax.random.normal(k2, (DIM, 3 * INNER), dtype=jnp.float32) * DIM ** (-0.5)
        W_out = jax.random.normal(k3, (INNER, DIM), dtype=jnp.float32) * INNER ** (-0.5)
        b_out = jax.random.normal(k4, (DIM,), dtype=jnp.float32) * 0.02
        return {'x': x, 'W_qkv': W_qkv, 'W_out': W_out, 'b_out': b_out}
    _L0_attn_all = _L0_attn_setup()
    _L0_attn_in = {k: v for k, v in _L0_attn_all.items() if k in ('W_qkv', 'W_out', 'b_out')}
    del _L0_attn_all

    def _L0_ffn_setup():
        import jax, jax.numpy as jnp
        import numpy as np
        B, T, D = (4, 2048, 128)
        E, F, CAP = (8, 512, 1024)
        key = jax.random.key(seed)
        ks = jax.random.split(key, 6)
        s = 0.02
        return {'x': jax.random.normal(ks[0], (B, T, D), dtype=jnp.float32), 'Wr': jax.random.normal(ks[1], (D, E), dtype=jnp.float32) * s, 'W1': jax.random.normal(ks[2], (E, D, F), dtype=jnp.float32) * s, 'b1': jax.random.normal(ks[3], (E, F), dtype=jnp.float32) * s, 'W2': jax.random.normal(ks[4], (E, F, D), dtype=jnp.float32) * s, 'b2': jax.random.normal(ks[5], (E, D), dtype=jnp.float32) * s}
    _L0_ffn_all = _L0_ffn_setup()
    _L0_ffn_in = {k: v for k, v in _L0_ffn_all.items() if k in ('Wr', 'W1', 'b1', 'W2', 'b2')}
    del _L0_ffn_all
    return {'x': x, 'L0_tok_w1': _L0_tok_in['w1'], 'L0_tok_b1': _L0_tok_in['b1'], 'L0_tok_w2': _L0_tok_in['w2'], 'L0_tok_b2': _L0_tok_in['b2'], 'L0_attn_W_qkv': _L0_attn_in['W_qkv'], 'L0_attn_W_out': _L0_attn_in['W_out'], 'L0_attn_b_out': _L0_attn_in['b_out'], 'L0_ffn_Wr': _L0_ffn_in['Wr'], 'L0_ffn_W1': _L0_ffn_in['W1'], 'L0_ffn_b1': _L0_ffn_in['b1'], 'L0_ffn_W2': _L0_ffn_in['W2'], 'L0_ffn_b2': _L0_ffn_in['b2']}

def reference(x, L0_tok_w1, L0_tok_b1, L0_tok_w2, L0_tok_b2, L0_attn_W_qkv, L0_attn_W_out, L0_attn_b_out, L0_ffn_Wr, L0_ffn_W1, L0_ffn_b1, L0_ffn_W2, L0_ffn_b2):
    import jax
    import jax.numpy as jnp

    def _L0_tok_ref(x, w1, b1, w2, b2):
        import jax, jax.numpy as jnp
        import numpy as np
        PATCH_SIZE = 200
        EMBED_DIM = 128
        IN_FEATURES = 2 * (PATCH_SIZE // 2 + 1)
        HIDDEN = 4 * IN_FEATURES
        B, C, T = x.shape
        P = PATCH_SIZE
        pad = -T % P
        if pad:
            x = jnp.pad(x, ((0, 0), (0, 0), (0, pad)))
            T = T + pad
        S = T // P
        xp = x.reshape(B, C, S, P)
        fr = jnp.fft.rfft(xp, axis=-1)
        feats = jnp.concatenate([jnp.abs(fr), jnp.angle(fr)], axis=-1)
        h = jax.nn.gelu(feats @ w1 + b1, approximate=False)
        out = h @ w2 + b2
        return out.reshape(B, C * S, EMBED_DIM)

    def _L0_attn_ref(x, W_qkv, W_out, b_out):
        import jax, jax.numpy as jnp
        import numpy as np
        HEADS = 8
        DIM_HEAD = 64
        SCALE = DIM_HEAD ** (-0.5)
        DIM = 128
        INNER = HEADS * DIM_HEAD

        def sparsemax(z):
            n = z.shape[-1]
            z_sorted = jnp.flip(jnp.sort(z, axis=-1), axis=-1)
            cssv = jnp.cumsum(z_sorted, axis=-1)
            r = jnp.arange(1, n + 1, dtype=z.dtype)
            support = 1.0 + r * z_sorted > cssv
            k = jnp.sum(support, axis=-1, keepdims=True)
            tau = (jnp.take_along_axis(cssv, k - 1, axis=-1) - 1.0) / k.astype(z.dtype)
            return jnp.maximum(z - tau, 0.0)
        B, N, _ = x.shape
        qkv = x @ W_qkv
        q, k, v = jnp.split(qkv, 3, axis=-1)

        def to_heads(t):
            return t.reshape(B, N, HEADS, DIM_HEAD).transpose(0, 2, 1, 3)
        q, k, v = (to_heads(q), to_heads(k), to_heads(v))
        sim = jnp.einsum('bhid,bhjd->bhij', q, k) * SCALE
        attn = sparsemax(sim)
        out = jnp.einsum('bhij,bhjd->bhid', attn, v)
        out = out.transpose(0, 2, 1, 3).reshape(B, N, INNER)
        return out @ W_out + b_out

    def _L0_ffn_ref(x, Wr, W1, b1, W2, b2):
        import jax, jax.numpy as jnp
        import numpy as np
        B, T, D = (4, 2048, 128)
        E, F, CAP = (8, 512, 1024)
        Bb, Tt, Dd = x.shape
        N = Bb * Tt
        C = min(CAP, N)
        x_flat = x.reshape(N, Dd)
        logits = x_flat @ Wr
        probs = jax.nn.softmax(logits, axis=0)
        vals, idx = jax.lax.top_k(probs.T, C)
        selected = x_flat[idx]
        h = jax.nn.gelu(jnp.einsum('ecd,edf->ecf', selected, W1) + b1[:, None, :], approximate=False)
        out_e = jnp.einsum('ecf,efd->ecd', h, W2) + b2[:, None, :]
        weighted = vals[..., None] * out_e
        output = jnp.zeros_like(x_flat).at[idx.reshape(-1)].add(weighted.reshape(-1, Dd))
        return output.reshape(Bb, Tt, Dd)
    h = _L0_tok_ref(x, L0_tok_w1, L0_tok_b1, L0_tok_w2, L0_tok_b2)
    h = h + _L0_attn_ref(_layernorm(h, axis=-1), L0_attn_W_qkv, L0_attn_W_out, L0_attn_b_out)
    h = h + _L0_ffn_ref(_layernorm(h, axis=-1), L0_ffn_Wr, L0_ffn_W1, L0_ffn_b1, L0_ffn_W2, L0_ffn_b2)
    return h

_drawn_inputs = setup_inputs


def setup_inputs(seed=0):
    import zlib

    import numpy as np

    out = dict(_drawn_inputs(seed))
    spreads = {}
    factors = {'L0_tok_b1': 6.599,
     'L0_tok_b2': 8.0,
     'L0_attn_b_out': 8.0,
     'L0_ffn_Wr': 64.0,
     'L0_ffn_W1': 64.0,
     'L0_ffn_b1': 64.0,
     'L0_ffn_W2': 64.0,
     'L0_ffn_b2': 64.0}
    for name, (base, spread) in spreads.items():
        noise = np.random.default_rng([zlib.crc32(name.encode()), seed]).standard_normal(out[name].shape)
        drawn = base * np.exp(spread * noise) if base else spread * noise
        out[name] = jnp.asarray(drawn.astype(out[name].dtype))
    for name, factor in factors.items():
        out[name] = (out[name] * factor).astype(out[name].dtype)
    return out
```

```python
import math
from contextlib import ExitStack

import numpy as np
import concourse.bass as bass
from concourse import mybir

ds = bass.ds


class Tally:

    def __init__(self, sem):
        self.sem, self.base, self.k = sem, 0, 0

    def up(self, n=1):
        self.k += n
        return self.base + self.k

    def now(self):
        return self.base + self.k

    def enter(self, i, start, per):
        self.start, self.per, self.outer = start, per, self.base + self.k
        self.base, self.k = self.outer + (i - start) * per, 0

    def leave(self, trips):
        assert self.k == self.per, (self.k, self.per)
        self.base, self.k = self.outer + trips * self.per, 0


class Counts:

    def __init__(self, sems):
        self.t = {n: Tally(s) for n, s in sems.items()}
        for n in sems:
            if n.startswith("free"):
                self.t[n].base = 1

    def up(self, name, n=1):
        return self.t[name].up(n)

    def now(self, name):
        return self.t[name].now()

    def enter(self, i, start, per):
        self.loop = per
        for n, k in per.items():
            self.t[n].enter(i, start, k)

    def at(self, name, k):
        return self.t[name].base + k

    def leave(self, trips):
        for n in self.loop:
            self.t[n].leave(trips)


def audio_tower(nc, x, tok_w1, tok_b1, tok_w2, tok_b2, w_qkv, w_out, b_out, w_r, e_w1, e_b1, e_w2, e_b2,
                cos_c, sin_c, out):
    f32, bf16, i32 = mybir.dt.float32, mybir.dt.bfloat16, mybir.dt.int32
    ALU, ACT, AX = mybir.AluOpType, mybir.ActivationFunctionType, mybir.AxisListType
    RMAX, RADD = bass.bass_isa.ReduceOp.max, bass.bass_isa.ReduceOp.add

    P = 128
    B, CH, T = x.shape
    PATCH = 200
    S = -(-T // PATCH)
    BINS = PATCH // 2 + 1
    HALF = PATCH // 2
    HID = tok_w1.shape[1]
    D = tok_w2.shape[1]
    MT = 7
    MW = -(-HID // MT)
    MS = [min(MW, HID - MW * m) for m in range(MT)]
    ROWS = B * CH
    XT = ROWS // P
    NTOK = ROWS * S
    NT = NTOK // P
    G = NTOK // 512
    SEQ = NTOK // B
    HEADS, DH = 8, 64
    INNER = HEADS * DH
    E = w_r.shape[1]
    F = e_w1.shape[2]
    CAP = min(1024, NTOK)
    CT = CAP // P
    EPS = 1e-5
    TINY = 1e-36
    SIGN, PI_BITS = -2147483648, 0x40490FDB
    LOWEST = -3.0e38

    rows2 = nc.dram_tensor("rows2", (NTOK, D), f32, kind="Internal").ap()

    ctx = ExitStack()
    with ctx:
        def sb(name, shape, dt=f32):
            return ctx.enter_context(nc.sbuf_tensor(name, shape, dt))

        def carve(name, words):
            area = sb(name, [P, words])

            def stage():
                at = [0]

                def cut(shape, dt=f32):
                    n = math.prod(shape[1:]) * (1 if dt != bf16 else 0.5)
                    lo = at[0]
                    at[0] += int(n)
                    assert at[0] <= words, (name, at[0])
                    v = area[0:shape[0], lo:at[0]]
                    if dt != f32:
                        v = v.bitcast(dt)
                    if len(shape) == 2:
                        return v
                    if len(shape) == 3:
                        return v.rearrange("p (a b) -> p a b", b=shape[2])
                    return v.rearrange("p (a b c) -> p a b c", b=shape[2], c=shape[3])
                return cut
            return stage

        front = carve("front", 17408)
        back = carve("back", 3 * NTOK)
        cut = front()
        x_cur = cut([P, 2, S * PATCH])
        even = cut([P, 2 * S, BINS])
        odd = cut([P, 2 * S, HALF - 1])
        even_t = cut([BINS, 1024])
        odd_t = cut([HALF - 1, 1024])
        re = cut([BINS, 1024])
        im = cut([BINS, 1024])
        re_sq = cut([BINS, 1024])
        im_sq = cut([BINS, 1024])
        mag_sq = cut([BINS, 1024])
        den = cut([BINS, 1024])
        cut = back()
        f_mag = cut([BINS, NTOK])
        f_ang = cut([BINS, NTOK])
        f_cor = cut([BINS, NTOK])
        cosb = sb("cosb", [BINS, BINS])
        sinb = sb("sinb", [HALF - 1, BINS])
        w1m = sb("w1m", [BINS, HID])
        w1a = sb("w1a", [BINS, HID])
        b1c = sb("b1c", [MW, MT])
        w2t = sb("w2t", [MW, MT, D])
        b2b = sb("b2b", [P, D])
        bob = sb("bob", [P, D])
        wqkv = sb("wqkv", [P, 3 * INNER])
        wo = sb("wo", [P, INNER // P, D])
        wr = sb("wr", [P, E])
        h = sb("h", [P, NT, D])
        hid = sb("hid", [MW, MT, 512])
        stats = sb("stats", [P, 4, 6])
        mv = sb("mv", [P, 4, 2])
        var_eps = sb("var_eps", [P, 4])
        rstd = sb("rstd", [P, 4])
        minus_half = sb("minus_half", [P, 4])
        xn = sb("xn", [P, 4, D])
        xn_t = sb("xn_t", [P, NTOK])
        cut = front()
        xcur = sb("xcur", [P, 512])
        qk = cut([P, 8, 512])
        v_sb = cut([P, 4, INNER])
        NS = 4
        sc = [cut([P, 4, SEQ]) for i in range(NS)]
        sc2 = cut([P, 4, SEQ])
        prob = [cut([P, 4, SEQ]) for i in range(2)]
        prob_t = [cut([P, 4, SEQ]) for i in range(2)]
        top = sb("top", [P, 4, 16])
        csum = sb("csum", [P, 4, 16])
        cand = sb("cand", [P, 4, 16])
        tau = sb("tau", [P, 2, 4])
        more = sb("more", [P, 2, 4])
        more_all = sb("more_all", [P, 2, 4])
        flag = sb("flag", [P, 2], i32)
        seg16 = sb("seg16", [P, 4, 16])
        inv16 = sb("inv16", [P, 4, 16])
        zeros = sb("zeros", [P, SEQ])
        r_sum = sb("r_sum", [P, 4])
        r_cnt = sb("r_cnt", [P, 4])
        go_w = sb("go_w", [P, 32])
        go_t = sb("go_t", [P, 32])
        go = sb("go", [P, 1], i32)
        o_sb = cut([P, 2, INNER])
        o_t = cut([P, 4, SEQ])
        ident = sb("ident", [P, P])
        x2_t = sb("x2_t", [P, 512])
        lg = sb("lg", [P, E, NT])
        pr = sb("pr", [P, E, NT])
        c8 = [sb(f"c8_{i}", [P, E]) for i in range(8)]
        BITS = 30
        thr = sb("thr", [P, E], i32)
        thr_c = sb("thr_c", [P, E], i32)
        bit_i = sb("bit_i", [P, E], i32)
        bit_f = sb("bit_f", [P, E])
        keep_b = sb("keep_b", [P, E], i32)
        ones = sb("ones", [P, P])
        before = sb("before", [P, P])
        seg32 = sb("seg32", [P, E, NT])
        cut = front()
        gt = cut([P, E, NT])
        eq = cut([P, E, NT])
        sel = sb("sel", [P, E, NT])
        tmp = cut([P, E, NT])
        tot = cut([P, E, NT])
        rank = cut([P, E, NT])
        rank_i = cut([P, E, NT], i32)
        lo_i = cut([P, E, NT], i32)
        hi_i = cut([P, E, NT], i32)
        lo_f = cut([P, E, NT])
        hi_f = cut([P, E, NT])
        iota_r = sb("iota_r", [P, P])
        iota_p = sb("iota_p", [P, 1])
        vals = cut([P, E, NT, 5])
        half16 = sb("half16", [P, E, NT], bf16)
        lo_hot = cut([P, NT, P], bf16)
        hi_hot = cut([P, NT, CT])
        hi_val = cut([P, NT, 5, CT], bf16)
        parts = sb("parts", [P, 5, CT])
        slot_f = sb("slot_f", [P, CT])
        slot_w = sb("slot_w", [P, E, CT])
        slot_i = sb("slot_i", [P, E, CT], i32)
        cut = back()
        ew1 = [cut([P, F]) for i in range(2)]
        ew2 = [cut([P, F // P, D]) for i in range(2)]
        eb1 = [sb(f"eb1_{i}", [P, F // P]) for i in range(2)]
        eb2 = [sb(f"eb2_{i}", [P, D]) for i in range(2)]
        idx = [sb(f"idx{i}", [P, CT], i32) for i in range(2)]
        xg = [cut([P, CT, D]) for i in range(2)]
        xg_t = cut([P, CAP])
        eh = cut([P, F // P, CAP])
        y = [cut([P, CT, D]) for i in range(2)]

        ps = [ctx.enter_context(nc.psum_tensor(f"ps{i}", [P, 1024], f32)) for i in range(4)]

        names = ["full0", "full1", "full2", "full3",
                 "free0", "free1", "free2", "free3",
                 "x_in", "tok_w_in", "att_w_in", "const", "fold", "fold_used", "re_ok", "im_ok", "sq_ok", "msq_ok",
                 "mag_ok", "ratio_ok", "atan_ok", "feat_ok", "ve_ok", "rstd_ok", "xn_ok", "xcur_ok",
                 "xcur_used", "relu_ok", "more_ok", "more_seen", "held", "anymore_ok", "top_ok", "h_ok", "rows_out", "x2_ok", "lg_ok",
                 "mx_in", "mx_ok", "ex_in", "ex_ok", "sm_in", "sm_ok", "cnt_in", "rk_in", "hot_ok",
                 "slots_ok", "ew_in0", "ew_in1", "xg_in0", "xg_in1", "xg_used", "y_ok", "y_out", "y_free", "ew_used"]
        sems = {n: ctx.enter_context(nc.semaphore(n)) for n in names}
        block = ctx.enter_context(nc.Block())

        def layernorm(v, c, tiles):
            v.drain()
            for j in range(4):
                v.bn_stats(stats[:, j, :], tiles[:, j, :])
            v.drain()
            for j in range(4):
                v.bn_aggr(mv[:, j, :], stats[:, j, :])
            v.drain()
            v.tensor_scalar(var_eps[:, :], mv[:, :, 1], EPS, None, ALU.add).then_inc(sems["ve_ok"], 1)
            v.wait_ge(sems["rstd_ok"], c.up("rstd_ok"))
            for j in range(4):
                last = v.tensor_scalar(xn[:, j, :], tiles[:, j, :], mv[:, j, 0:1], rstd[:, j:j + 1],
                                       ALU.subtract, ALU.mult)
            return last

        @block.sync
        def _(sp):
            c = Counts(sems)
            for n in ("free0", "free1", "free2", "free3", "fold_used", "ratio_ok", "xcur_used", "relu_ok",
                      "rows_out"):
                sp.sem_inc(sems[n], 1)
            xr = x.rearrange("b c t -> (b c) t")
            with sp.Fori(0, NTOK // 1024) as i:
                sp.wait_ge(sems["fold_used"], i + 1)
                sp.dma_start(x_cur[:, :, 0:T], xr[ds(i * (2 * P), 2 * P), :].rearrange("(t p) n -> p t n", p=P))\
                    .then_inc(sems["x_in"], 16)
            with sp.Fori(0, G) as t:
                c.enter(t, 0, {"xn_ok": 1})
                sp.wait_ge(sems["xn_ok"], c.up("xn_ok") + G)
                sp.dma_start(rows2[ds(t * 512, 512), :].rearrange("(j p) d -> p j d", p=P),
                             xn[:, :, :]).then_inc(sems["rows_out"], 16)
                c.leave(G)
            sp.dma_start(out.rearrange("b s d -> (b s) d").rearrange("(j p) d -> p j d", p=P),
                         h[:, :, :]).then_inc(sems["rows_out"], 16)
            with sp.Fori(0, E // 2) as n:
                for p in range(2):
                    e = n * 2
                    sp.wait_ge(sems["ew_used"], e + (p + 1))
                    sp.dma_start(ew1[p][:, :], e_w1[ds(e + p, 1), :, :].rearrange("e d f -> (e d) f"))\
                        .then_inc(sems[f"ew_in{p}"], 16)
                    sp.dma_start(ew2[p][:, :, :], e_w2[ds(e + p, 1), :, :].rearrange("e (k f) d -> f (e k) d", f=P))\
                        .then_inc(sems[f"ew_in{p}"], 16)
                    sp.dma_start(eb1[p][:, :], e_b1[ds(e + p, 1), :].rearrange("e (k f) -> f (e k)", f=P),
                                 allow_slow_non_contiguous=True).then_inc(sems[f"ew_in{p}"], 16)
                    sp.dma_start(eb2[p][:, :], e_b2[ds(e + p, 1), :].partition_broadcast(P))\
                        .then_inc(sems[f"ew_in{p}"], 16)
            sp.wait_ge(sems["y_out"], 16 * E * CT)

        @block.gpsimd
        def _(g):
            c = Counts(sems)
            g.memset(ident[:, :], 0.0)
            g.memset(ones[:, :], 1.0)
            g.memset(before[:, :], 1.0)
            g.memset(minus_half[:, :], -0.5)
            g.memset(zeros[:, :], 0.0)
            g.memset(seg16[:, :, :], 1.0)
            g.memset(seg32[:, :, :], 1.0)
            g.iota(iota_r[:, :], [[1, P]], base=0, channel_multiplier=0, allow_small_or_imprecise_dtypes=True)
            g.iota(iota_p[:, :], [[0, 1]], base=0, channel_multiplier=1, allow_small_or_imprecise_dtypes=True)
            g.drain()
            g.affine_select(out=ident[:, :], in_=ident[:, :], compare_op=ALU.not_equal, fill=1.0,
                            base=0, pattern=[[-1, P]], channel_multiplier=1)
            g.affine_select(out=before[:, :], in_=before[:, :], compare_op=ALU.is_gt, fill=0.0,
                            base=0, pattern=[[1, P]], channel_multiplier=-1)
            g.memset(seg16[:, :, 0:1], 0.0)
            g.memset(seg32[:, :, 0:1], 0.0)
            for n in range(16):
                g.memset(inv16[:, :, n:n + 1], 1.0 / (n + 1))
            g.drain()
            g.engine_nop().then_inc(sems["const"], 1)

            def power():
                g.wait_ge(sems["ve_ok"], c.up("ve_ok"))
                g.tensor_tensor(rstd[:, :], var_eps[:, :], minus_half[:, :], ALU.pow)\
                    .then_inc(sems["rstd_ok"], 1)

            with g.Fori(0, G) as t:
                c.enter(t, 0, {"ve_ok": 1})
                power()
                c.leave(G)
            g.wait_ge(sems["free3"], 1 + 4 + 2 * G)
            with g.Fori(0, G) as t:
                c.enter(t, 0, {"more_ok": 8})
                g.wait_ge(sems["xcur_used"], t + 1)
                g.tensor_copy(xcur[:, :], xn_t[:, ds(t * 512, 512)]).then_inc(sems["xcur_ok"], 1)
                for u in range(8):
                    g.wait_ge(sems["more_ok"], c.up("more_ok"))
                    g.sem_inc(sems["more_seen"], 1)
                    g.partition_all_reduce(more_all[:, u % 2, :], more[:, u % 2, :], P, RMAX)\
                        .then_inc(sems["anymore_ok"], 1)
                c.leave(G)
            with g.Fori(0, G) as t:
                c.enter(t, 0, {"ve_ok": 1})
                power()
                c.leave(G)
            g.wait_ge(sems["mx_in"], 1)
            g.partition_all_reduce(c8[1][:, :], c8[0][:, :], P, RMAX).then_inc(sems["mx_ok"], 1)
            g.wait_ge(sems["sm_in"], 1)
            g.partition_all_reduce(c8[3][:, :], c8[2][:, :], P, RADD).then_inc(sems["sm_ok"], 1)
            g.wait_ge(sems["rows_out"], 16 * (G + 1) + 1)
            g.wait_ge(sems["slots_ok"], E)
            orow = out.rearrange("b s d -> (b s) d")

            g.sem_inc(sems["y_free"], 1)

            def gather(e, p):
                g.wait_ge(sems["xg_used"], e + 1)
                g.tensor_copy(idx[p][:, :], slot_i[:, ds(e, 1), :].rearrange("p e s -> p (e s)"))
                g.drain()
                for s in range(CT):
                    g.indirect_dma_start(xg[p][:, s, :], None, rows2[:, :],
                                         bass.IndirectOffsetOnAxis(ap=idx[p][:, s:s + 1], axis=0))\
                        .then_inc(sems[f"xg_in{p}"], 16)

            def scatter(n, p):
                g.wait_ge(sems["y_ok"], n + 1)
                added(n)
                g.sem_inc(sems["y_free"], 1)
                for s in range(CT):
                    g.indirect_dma_start(orow[:, :], bass.IndirectOffsetOnAxis(ap=idx[p][:, s:s + 1], axis=0),
                                         y[p][:, s, :], None, compute_op=ALU.add)\
                        .then_inc(sems["y_out"], 16)

            def added(n):
                if not (type(n) is int and n == 0):
                    g.wait_ge(sems["y_out"], n * (16 * CT))

            def round_of_two(n):
                for p in range(2):
                    e = n * 2 + p
                    added(e)
                    gather(n * 2 + (p + 1), 1 - p)
                    scatter(e, p)

            gather(0, 0)
            round_of_two(0)
            with g.Fori(1, E // 2 - 1) as n:
                round_of_two(n)
            added(E - 2)
            gather(E - 1, 1)
            scatter(E - 2, 0)
            scatter(E - 1, 1)

        @block.scalar
        def _(a):
            c = Counts(sems)
            a.dma_start(cosb[:, :], cos_c).then_inc(sems["tok_w_in"], 16)
            a.dma_start(sinb[:, :], sin_c).then_inc(sems["tok_w_in"], 16)
            a.dma_start(w1m[:, :], tok_w1[0:BINS, :]).then_inc(sems["tok_w_in"], 16)
            a.dma_start(w1a[:, :], tok_w1[BINS:2 * BINS, :]).then_inc(sems["tok_w_in"], 16)
            for m in range(MT):
                a.dma_start(w2t[0:MS[m], m, :], tok_w2[m * MW:m * MW + MS[m], :]).then_inc(sems["tok_w_in"], 16)
                a.dma_start(b1c[0:MS[m], m:m + 1], tok_b1[m * MW:m * MW + MS[m]].rearrange("(p a) -> p a", a=1))\
                    .then_inc(sems["tok_w_in"], 16)
            a.dma_start(b2b[:, :], tok_b2.partition_broadcast(P)).then_inc(sems["tok_w_in"], 16)
            a.dma_start(bob[:, :], b_out.partition_broadcast(P)).then_inc(sems["tok_w_in"], 16)
            a.dma_start(wqkv[:, :], w_qkv).then_inc(sems["att_w_in"], 16)
            a.dma_start(wo[:, :, :], w_out.rearrange("(k p) d -> p k d", p=P)).then_inc(sems["att_w_in"], 16)
            a.dma_start(wr[:, :], w_r).then_inc(sems["att_w_in"], 16)

            def full(s):
                a.wait_ge(sems[f"full{s}"], c.up(f"full{s}"))

            with a.Fori(0, NTOK // 1024) as i:
                c.enter(i, 0, {"full0": 1, "full2": 1, "im_ok": 1, "msq_ok": 1})
                full(0)
                for t in range(2):
                    last = a.activation(
                        even_t[:, t * 512:(t + 1) * 512].rearrange("k (r s) -> k s r", s=S),
                        ps[0][0:BINS, t * 512:(t + 1) * 512].rearrange("k (s r) -> k s r", s=S), ACT.Copy)
                last.then_inc(sems["free0"], 1)
                full(2)
                a.wait_ge(sems["ratio_ok"], i + 1)
                a.activation(re[:, :], ps[2][0:BINS, :], ACT.Copy).then_inc(sems["re_ok"], 1)
                a.activation(re_sq[:, :], ps[2][0:BINS, :], ACT.Square).then_inc(sems["free2"], 1)
                a.wait_ge(sems["im_ok"], c.up("im_ok"))
                a.activation(im_sq[:, :], im[:, :], ACT.Square).then_inc(sems["sq_ok"], 1)
                a.wait_ge(sems["msq_ok"], c.up("msq_ok"))
                a.activation(f_mag[:, ds(i * 1024, 1024)], mag_sq[:, :], ACT.Sqrt).then_inc(sems["mag_ok"], 1)
                c.leave(NTOK // 1024)
            c.up("full1", NTOK // 1024)
            c.up("full3", NTOK // 1024)
            a.wait_ge(sems["ratio_ok"], NTOK // 1024 + 1)
            with a.Fori(0, G) as t:
                a.activation(f_ang[:, ds(t * 512, 512)], f_ang[:, ds(t * 512, 512)], ACT.Arctan)\
                    .then_inc(sems["atan_ok"], 1)

            def gelus():
                for m in range(MT):
                    s = m % 3
                    full(s)
                    a.activation(hid[0:MS[m], m, :], ps[s][0:MS[m], 0:512], ACT.Gelu,
                                 bias=b1c[0:MS[m], m:m + 1]).then_inc(sems[f"free{s}"], 1)

            def columns(t):
                full(3)
                a.activation(xn_t[:, ds(t * 512, 512)], ps[3][:, 0:512], ACT.Copy).then_inc(sems["free3"], 1)

            a.wait_ge(sems["tok_w_in"], 16 * (6 + 2 * MT))
            gelus()
            c.up("full3")
            with a.Fori(1, G) as t:
                c.enter(t, 1, {"full0": 3, "full1": 2, "full2": 2, "full3": 2})
                gelus()
                columns(t - 1)
                c.up("full3")
                c.leave(G - 1)
            columns(G - 1)

            def empty(s, dst, src, scale=1.0):
                full(s)
                a.activation(dst, src, ACT.Copy, scale=scale).then_inc(sems[f"free{s}"], 1)

            with a.Fori(0, G) as t:
                c.enter(t, 0, {"full0": 9, "full1": 9, "full2": 8, "full3": 2, "relu_ok": 8})
                job = [0]

                def slot():
                    job[0] += 1
                    return (job[0] - 1) % 3

                for j in range(4):
                    s = slot()
                    empty(s, qk[:, 2 * j:2 * j + 2, :].rearrange("p a n -> p (a n)"), ps[s][:, :],
                          DH ** -0.5 if j < 2 else 1.0)
                for j in range(2):
                    s = slot()
                    empty(s, v_sb[:, 2 * j:2 * j + 2, :].rearrange("p a n -> p (a n)"), ps[s][:, :])

                def scores(u):
                    s = slot()
                    a.wait_ge(sems["relu_ok"], t * 8 + (max(u - NS + 1, 0) + 1))
                    empty(s, sc[u % NS][:, :, :].rearrange("p a n -> p (a n)"), ps[s][:, :])

                scores(0)
                scores(1)
                for u in range(8):
                    if u + 2 < 8:
                        scores(u + 2)
                    s = slot()
                    empty(s, prob_t[u % 2][:, :, :].rearrange("p a n -> p (a n)"), ps[s][:, :])
                    if u in (4, 7):
                        if u == 7:
                            empty(3, o_sb[:, :, :].rearrange("p a n -> p (a n)"), ps[3][:, :])
                        s = slot()
                        empty(s, o_t[:, :, :].rearrange("p a n -> p (a n)"), ps[s][:, :])
                        s = slot()
                        c.up(f"full{s}")
                    if u == 3:
                        empty(3, o_sb[:, :, :].rearrange("p a n -> p (a n)"), ps[3][:, :])
                c.up("relu_ok", 8)
                c.leave(G)
            with a.Fori(0, G) as t:
                c.enter(t, 0, {"full0": 1, "full1": 1})
                full(0)
                a.activation(x2_t[:, :], ps[0][:, 0:512], ACT.Copy).then_inc(sems["free0"], 1)
                c.up("full1")
                c.leave(G)

            a.wait_ge(sems["ex_in"], 1)
            a.activation(pr[:, :, :], lg[:, :, :], ACT.Exp).then_inc(sems["ex_ok"], 1)
            c.up("full0", BITS + 3 + E // 2)
            c.up("full1", E // 2)

            def expert_columns():
                full(2)
                a.activation(xg_t[:, :], ps[2][:, :], ACT.Copy).then_inc(sems["free2"], 1)

            def expert_gelus(n, p):
                a.wait_ge(sems[f"ew_in{p}"], (n + 1) * 64)
                for m in range(F // P):
                    s = m % 2
                    full(s)
                    a.activation(eh[:, m, :], ps[s][:, :], ACT.Gelu, bias=eb1[p][:, m:m + 1])\
                        .then_inc(sems[f"free{s}"], 1)

            expert_columns()
            with a.Fori(0, E // 2 - 1) as n:
                c.enter(n, 0, {"full0": 4, "full1": 4, "full2": 2})
                for p in range(2):
                    expert_gelus(n, p)
                    expert_columns()
                c.leave(E // 2 - 1)
            expert_gelus(E // 2 - 1, 0)
            expert_columns()
            expert_gelus(E // 2 - 1, 1)

        @block.tensor
        def _(t_):
            c = Counts(sems)
            free = c.up

            def start(s, before_me=None):
                t_.wait_ge(sems[f"free{s}"], c.now(f"free{s}"))

            def done(s, ins):
                ins.then_inc(sems[f"full{s}"], 1)
                c.up(f"free{s}")

            mm = nc.tensor.matmul
            t_.sem_inc(sems["xg_used"], 2)
            t_.wait_ge(sems["const"], 1)
            t_.wait_ge(sems["tok_w_in"], 16 * (6 + 2 * MT))
            t_.wait_ge(sems["att_w_in"], 48)
            with t_.Fori(0, NTOK // 1024) as i:
                c.enter(i, 0, {"fold": 2, "free0": 1, "free1": 1, "free2": 1, "free3": 1})
                for s, (src, k) in enumerate(((even, BINS), (odd, HALF - 1))):
                    t_.wait_ge(sems["fold"], c.up("fold"))
                    start(s)
                    for q in range(2 * S):
                        last = nc.tensor.transpose(ps[s][0:k, q * P:(q + 1) * P], src[:, q, :], ident[:, :])
                    done(s, last)
                for s, (basis, cols) in ((2, (cosb, even_t)), (3, (sinb, odd_t))):
                    start(s - 2)
                    start(s)
                    for q in range(2):
                        last = mm(ps[s][0:BINS, q * 512:(q + 1) * 512], basis[:, :], cols[:, q * 512:(q + 1) * 512],
                                  start=True, stop=True)
                    done(s, last)
                c.leave(NTOK // 1024)

            def hidden(t):
                t_.wait_ge(sems["feat_ok"], t + 1)
                for m in range(MT):
                    s = m % 3
                    start(s)
                    for w, f in ((w1m, f_mag), (w1a, f_ang)):
                        last = mm(ps[s][0:MS[m], 0:512], w[:, m * MW:m * MW + MS[m]], f[:, ds(t * 512, 512)],
                                  start=(w is w1m), stop=(w is w1a))
                    done(s, last)

            def embed():
                start(3)
                for s in range(3):
                    start(s)
                for j in range(4):
                    for m in range(MT):
                        last = mm(ps[3][:, j * D:(j + 1) * D], hid[0:MS[m], m, j * P:(j + 1) * P],
                                  w2t[0:MS[m], m, :], start=(m == 0), stop=(m == MT - 1))
                done(3, last)

            def columns(t, s):
                t_.wait_ge(sems["xn_ok"], t + 1)
                start(s)
                for j in range(4):
                    last = nc.tensor.transpose(ps[s][:, j * P:(j + 1) * P], xn[:, j, :], ident[:, :])
                done(s, last)

            hidden(0)
            embed()
            with t_.Fori(1, G) as t:
                c.enter(t, 1, {"free0": 3, "free1": 2, "free2": 2, "free3": 2})
                hidden(t)
                columns(t - 1, 3)
                embed()
                c.leave(G - 1)
            columns(G - 1, 3)

            with t_.Fori(0, G) as t:
                c.enter(t, 0, {"free0": 9, "free1": 9, "free2": 8, "free3": 2, "top_ok": 8})
                job = [0]

                def slot():
                    job[0] += 1
                    start((job[0] - 1) % 3)
                    return (job[0] - 1) % 3

                t_.wait_ge(sems["xcur_ok"], t + 1)
                for j in range(4):
                    s = slot()
                    for q in range(2):
                        m = 2 * j + q
                        last = mm(ps[s][:, q * 512:(q + 1) * 512], wqkv[:, m * P:(m + 1) * P], xcur[:, :],
                                  start=True, stop=True)
                    done(s, last)
                for j in range(2):
                    s = slot()
                    for q in range(2):
                        last = mm(ps[s][:, q * 512:(q + 1) * 512], xcur[:, (2 * j + q) * P:(2 * j + q + 1) * P],
                                  wqkv[:, 2 * INNER:3 * INNER], start=True, stop=True)
                    done(s, last)
                last = None
                for s in range(3):
                    start(s)
                t_.sem_inc(sems["xcur_used"], 1)

                def scores(u):
                    b, hp = divmod(u, 4)
                    s = slot()
                    for it in range(2):
                        for a_ in range(2):
                            r = slice(a_ * DH, (a_ + 1) * DH)
                            last = mm(ps[s][:, a_ * 512 + it * SEQ:a_ * 512 + (it + 1) * SEQ],
                                      qk[r, hp, b * SEQ + it * P:b * SEQ + (it + 1) * P],
                                      qk[r, 4 + hp, b * SEQ:(b + 1) * SEQ], start=True, stop=True)
                    done(s, last)

                def mix(u):
                    b, hp = divmod(u, 4)
                    s = slot()
                    t_.wait_ge(sems["top_ok"], c.up("top_ok"))
                    for a_ in range(2):
                        for jb in range(2):
                            for it in range(2):
                                last = nc.tensor.transpose(
                                    ps[s][:, a_ * 512 + jb * SEQ + it * P:a_ * 512 + jb * SEQ + (it + 1) * P],
                                    prob[u % 2][:, 2 * a_ + it, jb * P:(jb + 1) * P], ident[:, :])
                    done(s, last)
                    if hp == 0:
                        start(3)
                    start(s)
                    for it in range(2):
                        for a_ in range(2):
                            hd = 2 * hp + a_
                            for jb in range(2):
                                last = mm(ps[3][:, it * 512 + hd * DH:it * 512 + (hd + 1) * DH],
                                          prob_t[u % 2][:, 2 * a_ + jb, it * P:(it + 1) * P],
                                          v_sb[:, 2 * b + jb, hd * DH:(hd + 1) * DH], start=(jb == 0), stop=(jb == 1))
                    if hp == 3:
                        done(3, last)

                def project():
                    start(3)
                    s = slot()
                    for k in range(4):
                        for it in range(2):
                            last = nc.tensor.transpose(ps[s][:, k * SEQ + it * P:k * SEQ + (it + 1) * P],
                                                       o_sb[:, it, k * P:(k + 1) * P], ident[:, :])
                    done(s, last)
                    start(s)
                    s = slot()
                    for it in range(2):
                        for k in range(4):
                            last = mm(ps[s][:, it * D:(it + 1) * D], o_t[:, k, it * P:(it + 1) * P], wo[:, k, :],
                                      start=(k == 0), stop=(k == 3))
                    done(s, last)

                scores(0)
                scores(1)
                for u in range(8):
                    if u + 2 < 8:
                        scores(u + 2)
                    mix(u)
                    if u in (4, 7):
                        project()
                c.leave(G)

            with t_.Fori(0, G) as t:
                c.enter(t, 0, {"free0": 1, "free1": 1})
                columns(t + G, 0)
                start(0)
                start(1)
                for j in range(4):
                    last = mm(ps[1][:, j * E:(j + 1) * E], x2_t[:, j * P:(j + 1) * P], wr[:, :], start=True, stop=True)
                done(1, last)
                c.leave(G)

            def total(n):
                t_.wait_ge(sems["cnt_in"], n + 1)
                start(0)
                done(0, mm(ps[0][:, 0:E], ones[:, :], c8[4][:, :], start=True, stop=True))

            with t_.Fori(0, BITS) as n:
                c.enter(n, 0, {"free0": 1})
                total(n)
                c.leave(BITS)
            total(BITS)
            for n, m in enumerate((eq, sel)):
                t_.wait_ge(sems["rk_in"], n + 1)
                start(0)
                mm(ps[0][:, 0:E * NT], before[:, :], m[:, :, :].rearrange("p e j -> p (e j)"), start=True, stop=True)
                done(0, mm(ps[0][:, 512:512 + E * NT], ones[:, :], m[:, :, :].rearrange("p e j -> p (e j)"),
                           start=True, stop=True))
            with t_.Fori(0, E // 2) as n:
                c.enter(n, 0, {"free0": 1, "free1": 1})
                for p in range(2):
                    t_.wait_ge(sems["hot_ok"], n * 2 + (p + 1))
                    start(p)
                    for j in range(NT):
                        last = mm(ps[p][:, 0:5 * CT], lo_hot[:, j, :],
                                  hi_val[:, j, :, :].rearrange("p v s -> p (v s)"), start=(j == 0), stop=(j == NT - 1))
                    done(p, last)
                c.leave(E // 2)

            def expert_columns(n, p):
                t_.wait_ge(sems[f"xg_in{p}"], (n + 1) * (16 * CT))
                start(2)
                for s in range(CT):
                    last = nc.tensor.transpose(ps[2][:, s * P:(s + 1) * P], xg[p][:, s, :], ident[:, :])
                done(2, last)
                t_.sem_inc(sems["xg_used"], 1)

            def expert_hidden(n, p):
                t_.wait_ge(sems[f"ew_in{p}"], (n + 1) * 64)
                start(2)
                for m in range(F // P):
                    s = m % 2
                    start(s)
                    for q in range(CAP // 512):
                        last = mm(ps[s][:, q * 512:(q + 1) * 512], ew1[p][:, m * P:(m + 1) * P],
                                  xg_t[:, q * 512:(q + 1) * 512], start=True, stop=True)
                    done(s, last)

            def expert_out(p):
                for s in (0, 1, 3):
                    start(s)
                for s in range(CT):
                    for k in range(F // P):
                        last = mm(ps[3][:, s * D:(s + 1) * D], eh[:, k, s * P:(s + 1) * P], ew2[p][:, k, :],
                                  start=(k == 0), stop=(k == F // P - 1))
                done(3, last)

            expert_columns(0, 0)
            with t_.Fori(0, E // 2 - 1) as n:
                c.enter(n, 0, {"free0": 4, "free1": 4, "free2": 2, "free3": 2})
                for p in range(2):
                    expert_hidden(n, p)
                    expert_columns(n + p, 1 - p)
                    expert_out(p)
                c.leave(E // 2 - 1)
            expert_hidden(E // 2 - 1, 0)
            expert_columns(E // 2 - 1, 1)
            expert_out(0)
            expert_hidden(E // 2 - 1, 1)
            expert_out(1)

        @block.vector
        def _(v):
            c = Counts(sems)

            def full(s):
                v.wait_ge(sems[f"full{s}"], c.up(f"full{s}"))

            def skip(*slots):
                for s in slots:
                    c.up(f"full{s}")

            v.sem_inc(sems["ew_used"], 2)
            v.wait_ge(sems["const"], 1)
            v.memset(x_cur[:, :, T:S * PATCH], 0.0)
            v.drain()

            with v.Fori(0, NTOK // 1024) as i:
                c.enter(i, 0, {"full0": 1, "full1": 1, "full2": 1, "full3": 1, "re_ok": 1, "sq_ok": 1, "mag_ok": 1})
                xv = x_cur[:, :, :].rearrange("p t (s n) -> p (t s) n", n=PATCH)
                v.wait_ge(sems["x_in"], (i + 1) * 16)
                v.tensor_copy(even[:, :, 0:BINS:HALF], xv[:, :, 0:BINS:HALF])
                v.tensor_tensor(even[:, :, 1:HALF], xv[:, :, 1:HALF], xv[:, :, PATCH - 1:HALF:-1], ALU.add)\
                    .then_inc(sems["fold"], 1)
                v.tensor_tensor(odd[:, :, :], xv[:, :, 1:HALF], xv[:, :, PATCH - 1:HALF:-1], ALU.subtract)\
                    .then_inc(sems["fold"], 1)
                v.drain().then_inc(sems["fold_used"], 1)
                skip(0)
                full(1)
                for t in range(2):
                    last = v.tensor_copy(
                        odd_t[:, t * 512:(t + 1) * 512].rearrange("k (r s) -> k s r", s=S),
                        ps[1][0:HALF - 1, t * 512:(t + 1) * 512].rearrange("k (s r) -> k s r", s=S))
                last.then_inc(sems["free1"], 1)
                full(3)
                v.tensor_scalar(im[:, :], ps[3][0:BINS, :], 0.0, None, ALU.add).then_inc(sems["free3"], 1)
                v.drain().then_inc(sems["im_ok"], 1)
                v.tensor_scalar(den[:, :].bitcast(i32), im[:, :].bitcast(i32), SIGN, PI_BITS,
                                ALU.bitwise_and, ALU.bitwise_or)
                skip(2)
                v.drain()
                v.wait_ge(sems["re_ok"], c.up("re_ok"))
                v.scalar_tensor_tensor(f_cor[:, ds(i * 1024, 1024)], re[:, :], 0.0, den[:, :], ALU.is_lt, ALU.mult)
                v.wait_ge(sems["sq_ok"], c.up("sq_ok"))
                v.scalar_tensor_tensor(mag_sq[:, :], re_sq[:, :], TINY, im_sq[:, :], ALU.add, ALU.add)\
                    .then_inc(sems["msq_ok"], 1)
                v.wait_ge(sems["mag_ok"], c.up("mag_ok"))
                fm = f_mag[:, ds(i * 1024, 1024)]
                v.scalar_tensor_tensor(den[:, :].bitcast(i32), re[:, :].bitcast(i32), SIGN, fm.bitcast(i32),
                                       ALU.bitwise_and, ALU.bitwise_or)
                v.drain()
                v.tensor_tensor(den[:, :], den[:, :], re[:, :], ALU.add)
                v.drain()
                v.reciprocal(den[:, :], den[:, :])
                v.drain()
                v.tensor_tensor(f_ang[:, ds(i * 1024, 1024)], im[:, :], den[:, :], ALU.mult)\
                    .then_inc(sems["ratio_ok"], 1)
                c.leave(NTOK // 1024)
            with v.Fori(0, G) as t:
                v.wait_ge(sems["atan_ok"], t + 1)
                fa = f_ang[:, ds(t * 512, 512)]
                v.scalar_tensor_tensor(fa, fa, 2.0, f_cor[:, ds(t * 512, 512)], ALU.mult, ALU.add)\
                    .then_inc(sems["feat_ok"], 1)

            v.wait_ge(sems["tok_w_in"], 16 * (6 + 2 * MT))

            def embeddings(t):
                skip(0, 0, 0, 1, 1, 2, 2)
                full(3)
                tiles = h[:, ds(t * 4, 4), :]
                v.tensor_tensor(tiles, ps[3][:, 0:512].rearrange("p (j d) -> p j d", d=D),
                                b2b[:, :].unsqueeze(1).to_broadcast([P, 4, D]), ALU.add).then_inc(sems["free3"], 1)
                layernorm(v, c, tiles).then_inc(sems["xn_ok"], 1)
                v.drain()
                v.tensor_tensor(tiles, tiles, bob[:, :].unsqueeze(1).to_broadcast([P, 4, D]), ALU.add)

            embeddings(0)
            with v.Fori(1, G) as t:
                c.enter(t, 1, {"full0": 3, "full1": 2, "full2": 2, "full3": 2, "rstd_ok": 1})
                skip(3)
                embeddings(t)
                c.leave(G - 1)
            skip(3)

            def top16(u):
                z, q = sc[u % NS], u % 2
                for r in range(4):
                    v.max(top[:, r, 0:8], z[:, r, :])
                v.drain()
                for r in range(4):
                    v.match_replace(sc2[:, r, :], top[:, r, 0:8], z[:, r, :], LOWEST)
                v.drain()
                for r in range(4):
                    v.max(top[:, r, 8:16], sc2[:, r, :])
                v.drain()
                v.tensor_tensor_scan(csum[:, :, :].rearrange("p r n -> p (r n)"), seg16[:, :, :].rearrange("p r n -> p (r n)"),
                                     top[:, :, :].rearrange("p r n -> p (r n)"), 0.0, ALU.mult, ALU.add)
                v.drain()
                v.scalar_tensor_tensor(cand[:, :, :], csum[:, :, :], -1.0, inv16[:, :, :], ALU.add, ALU.mult)
                v.drain()
                v.tensor_reduce(tau[:, q, :], cand[:, :, :], AX.X, ALU.max)
                v.drain()
                v.tensor_tensor(more[:, q, :], top[:, :, 15], tau[:, q, :], ALU.is_gt).then_inc(sems["more_ok"], 1)

            def newton(u):
                z, q = sc[u % NS], u % 2
                for r in range(4):
                    v.scalar_tensor_tensor(sc2[:, r, :], z[:, r, :], tau[:, q, r:r + 1], zeros[:, :],
                                           ALU.subtract, ALU.max, accum_out=r_sum[:, r:r + 1])
                    v.drain()
                    v.tensor_scalar(sc2[:, r, :], z[:, r, :], tau[:, q, r:r + 1], None, ALU.is_gt, ALU.add,
                                    accum_out=r_cnt[:, r:r + 1])
                    v.drain()
                v.tensor_scalar(r_sum[:, :], r_sum[:, :], -1.0, None, ALU.add)
                v.tensor_scalar(r_cnt[:, :], r_cnt[:, :], 1.0, None, ALU.max)
                v.drain()
                v.reciprocal(r_cnt[:, :], r_cnt[:, :])
                v.tensor_reduce(go_w[:, 0:1], r_sum[:, :], AX.X, ALU.max)
                v.drain()
                v.tensor_tensor(r_cnt[:, :], r_sum[:, :], r_cnt[:, :], ALU.mult)
                v.drain()
                v.tensor_tensor(tau[:, q, :], tau[:, q, :], r_cnt[:, :], ALU.add)
                v.transpose(go_t[:, :], go_w[:, :])
                v.drain()
                v.tensor_reduce(r_sum[:, 0:1], go_t[:, :], AX.X, ALU.max)
                v.drain()
                v.tensor_scalar(go[:, :], r_sum[:, 0:1], 3e-6, None, ALU.is_gt)
                v.drain()

            def probabilities(u):
                z, q = sc[u % NS], u % 2
                v.wait_ge(sems["anymore_ok"], c.up("anymore_ok"))
                v.sem_inc(sems["held"], 1)
                v.drain()
                v.tensor_reduce(flag[:, q:q + 1], more_all[:, q, :], AX.X, ALU.max)
                v.drain()
                wanted = v.value_load(flag[0:1, q:q + 1], min_val=0, max_val=1)
                with v.If(wanted > 0):
                    newton(u)
                    with v.Fori(0, 23):
                        left = [v.value_load(go[32 * k:32 * k + 1, 0:1], min_val=0, max_val=1) for k in range(4)]
                        with v.If(left[0] + left[1] + left[2] + left[3] > 0):
                            newton(u)
                for r in range(4):
                    last = v.tensor_scalar(prob[u % 2][:, r, :], z[:, r, :], tau[:, q, r:r + 1], 0.0,
                                           ALU.subtract, ALU.max)
                v.drain().then_inc(sems["top_ok"], 1)
                v.sem_inc(sems["relu_ok"], 1)

            v.memset(go_w[:, :], 0.0)
            for s, n in enumerate((3, 2, 2, 2)):
                c.up(f"free{s}", NTOK // 1024 + G * n)
            jobs = ["q", "q", "k", "k", "v", "v", "score0", "score1"]
            for u in range(8):
                jobs += [f"score{u + 2}"] * (u + 2 < 8) + [f"mix{u}"] + ["heads", f"project{u // 7}"] * (u in (4, 7))
            with v.Fori(0, G) as t:
                per = {"full0": 9, "full1": 9, "full2": 8, "full3": 2, "free0": 9, "free1": 9, "free2": 8, "free3": 2}
                c.enter(t, 0, {**per, "anymore_ok": 8})

                def scored(u):
                    n = jobs.index(f"score{u}")
                    v.wait_ge(sems[f"free{n % 3}"], c.at(f"free{n % 3}", n // 3 + 1))
                    v.sem_inc(sems["held"], 1)
                    v.drain()

                def residual(b):
                    n = jobs.index(f"project{b}")
                    v.wait_ge(sems[f"full{n % 3}"], c.at(f"full{n % 3}", n // 3 + 1))
                    tiles = h[:, ds(t * 4 + 2 * b, 2), :]
                    v.tensor_tensor(tiles, tiles, ps[n % 3][:, 0:2 * D].rearrange("p (j d) -> p j d", d=D), ALU.add)\
                        .then_inc(sems[f"free{n % 3}"], 1)

                scored(0)
                top16(0)
                for u in range(8):
                    if u < 7:
                        scored(u + 1)
                        top16(u + 1)
                    if u >= 2:
                        n = jobs.index(f"mix{u - 2}")
                        v.wait_ge(sems[f"full{n % 3}"], c.at(f"full{n % 3}", n // 3 + 1))
                    probabilities(u)
                    if u == 6:
                        residual(0)
                residual(1)
                for n, k in per.items():
                    c.up(n, k)
                c.leave(G)

            with v.Fori(0, G) as t:
                c.enter(t, 0, {"full0": 1, "full1": 1, "rstd_ok": 1})
                v.wait_ge(sems["rows_out"], t * 16 + 1)
                v.sem_inc(sems["held"], 1)
                layernorm(v, c, h[:, ds(t * 4, 4), :]).then_inc(sems["xn_ok"], 1)
                skip(0)
                full(1)
                v.tensor_copy(lg[:, :, ds(t * 4, 4)].rearrange("p e j -> p j e"),
                              ps[1][:, 0:4 * E].rearrange("p (j e) -> p j e", e=E)).then_inc(sems["free1"], 1)
                c.leave(G)

            def over_tokens(m):
                return m[:, :].unsqueeze(2).to_broadcast([P, E, NT])

            def flat(m):
                return m[:, :, :].rearrange("p e j -> p (e j)")

            v.drain()
            v.tensor_reduce(c8[0][:, :], lg[:, :, :], AX.X, ALU.max).then_inc(sems["mx_in"], 1)
            v.wait_ge(sems["mx_ok"], 1)
            v.tensor_tensor(lg[:, :, :], lg[:, :, :], over_tokens(c8[1]), ALU.subtract).then_inc(sems["ex_in"], 1)
            v.wait_ge(sems["ex_ok"], 1)
            v.tensor_reduce(c8[2][:, :], pr[:, :, :], AX.X, ALU.add).then_inc(sems["sm_in"], 1)
            v.wait_ge(sems["sm_ok"], 1)
            v.reciprocal(c8[3][:, :], c8[3][:, :])
            v.memset(thr[:, :], 0)
            v.memset(bit_i[:, :], 1 << (BITS - 1))
            v.memset(bit_f[:, :], float(1 << (BITS - 1)))
            v.drain()
            v.tensor_tensor(pr[:, :, :], pr[:, :, :], over_tokens(c8[3]), ALU.mult)

            def count(mask):
                v.drain()
                v.tensor_reduce(c8[4][:, :], mask[:, :, :], AX.X, ALU.add).then_inc(sems["cnt_in"], 1)
                full(0)

            with v.Fori(0, BITS) as n:
                c.enter(n, 0, {"full0": 1})
                v.drain()
                v.tensor_tensor(thr_c[:, :], thr[:, :], bit_i[:, :], ALU.bitwise_or)
                v.drain()
                v.tensor_tensor(tmp[:, :, :], pr[:, :, :],
                                thr_c[:, :].bitcast(f32).unsqueeze(2).to_broadcast([P, E, NT]), ALU.is_ge)
                count(tmp)
                v.scalar_tensor_tensor(keep_b[:, :], ps[0][:, 0:E], float(CAP), bit_f[:, :], ALU.is_ge, ALU.mult)\
                    .then_inc(sems["free0"], 1)
                v.drain()
                v.tensor_tensor(thr[:, :], thr[:, :], keep_b[:, :], ALU.bitwise_or)
                v.tensor_scalar(bit_i[:, :], bit_i[:, :], 1, None, ALU.logical_shift_right)
                v.tensor_scalar(bit_f[:, :], bit_f[:, :], 0.5, None, ALU.mult)
                c.leave(BITS)
            v.drain()
            thr_b = thr[:, :].bitcast(f32).unsqueeze(2).to_broadcast([P, E, NT])
            v.tensor_tensor(gt[:, :, :], pr[:, :, :], thr_b, ALU.is_gt)
            v.tensor_tensor(eq[:, :, :], pr[:, :, :], thr_b, ALU.is_equal)
            count(gt)
            v.tensor_scalar(c8[5][:, :], ps[0][:, 0:E], -1.0, float(CAP), ALU.mult, ALU.add).then_inc(sems["free0"], 1)

            def ranks(mask):
                v.drain().then_inc(sems["rk_in"], 1)
                full(0)
                v.tensor_copy(flat(tot), ps[0][:, 512:512 + E * NT])
                v.drain()
                v.tensor_tensor_scan(flat(rank), flat(seg32), flat(tot), 0.0, ALU.mult, ALU.add)
                v.drain()
                v.tensor_tensor(flat(rank), flat(rank), flat(tot), ALU.subtract)
                v.drain()
                v.tensor_tensor(flat(rank), flat(rank), ps[0][:, 0:E * NT], ALU.add).then_inc(sems["free0"], 1)
                v.drain()

            ranks(eq)
            v.tensor_tensor(tmp[:, :, :], rank[:, :, :], over_tokens(c8[5]), ALU.is_lt)
            v.drain()
            v.tensor_tensor(eq[:, :, :], eq[:, :, :], tmp[:, :, :], ALU.mult)
            v.drain()
            v.tensor_tensor(sel[:, :, :], eq[:, :, :], gt[:, :, :], ALU.add)
            ranks(sel)
            v.tensor_copy(rank_i[:, :, :], rank[:, :, :])
            v.drain()
            v.tensor_scalar(lo_i[:, :, :], rank_i[:, :, :], P - 1, None, ALU.bitwise_and)
            v.tensor_scalar(hi_i[:, :, :], rank_i[:, :, :], int(math.log2(P)), None, ALU.logical_shift_right)
            v.drain()
            v.tensor_copy(lo_f[:, :, :], lo_i[:, :, :])
            v.tensor_copy(hi_f[:, :, :], hi_i[:, :, :])
            v.tensor_copy(vals[:, :, :, 0], iota_r[:, 0:NT].unsqueeze(1).to_broadcast([P, E, NT]))
            v.tensor_copy(vals[:, :, :, 1], iota_p[:, :].unsqueeze(1).to_broadcast([P, E, NT]))
            v.tensor_copy(half16[:, :, :], pr[:, :, :])
            v.drain()
            v.tensor_copy(vals[:, :, :, 2], half16[:, :, :])
            v.drain()
            v.tensor_tensor(tmp[:, :, :], pr[:, :, :], vals[:, :, :, 2], ALU.subtract)
            v.drain()
            v.tensor_copy(half16[:, :, :], tmp[:, :, :])
            v.drain()
            v.tensor_copy(vals[:, :, :, 3], half16[:, :, :])
            v.drain()
            v.tensor_tensor(vals[:, :, :, 4], tmp[:, :, :], vals[:, :, :, 3], ALU.subtract)
            v.drain()

            def one_hots(e):
                lo = lo_f[:, ds(e, 1), :].rearrange("p e j -> p (e j)")
                hi = hi_f[:, ds(e, 1), :].rearrange("p e j -> p (e j)")
                on = sel[:, ds(e, 1), :].rearrange("p e j -> p (e j)")
                va = vals[:, ds(e, 1), :, :].rearrange("p e j n -> p (e j) n")
                v.tensor_tensor(lo_hot[:, :, :], iota_r[:, :].unsqueeze(1).to_broadcast([P, NT, P]),
                                lo.unsqueeze(2).to_broadcast([P, NT, P]), ALU.is_equal)
                v.tensor_tensor(hi_hot[:, :, :], iota_r[:, 0:CT].unsqueeze(1).to_broadcast([P, NT, CT]),
                                hi.unsqueeze(2).to_broadcast([P, NT, CT]), ALU.is_equal)
                v.drain()
                v.tensor_tensor(hi_hot[:, :, :], hi_hot[:, :, :], on.unsqueeze(2).to_broadcast([P, NT, CT]), ALU.mult)
                v.drain()
                for n in range(5):
                    v.tensor_tensor(hi_val[:, :, n, :], hi_hot[:, :, :],
                                    va[:, :, n].unsqueeze(2).to_broadcast([P, NT, CT]), ALU.mult)
                v.drain().then_inc(sems["hot_ok"], 1)

            with v.Fori(0, E // 2) as n:
                c.enter(n, 0, {"full0": 1, "full1": 1})
                for p in range(2):
                    e = n * 2 + p
                    one_hots(e)
                    full(p)
                    v.tensor_copy(parts[:, :, :].rearrange("p v s -> p (v s)"), ps[p][:, 0:5 * CT])\
                        .then_inc(sems[f"free{p}"], 1)
                    v.drain()
                    v.scalar_tensor_tensor(slot_f[:, :], parts[:, 0, :], float(P), parts[:, 1, :], ALU.mult, ALU.add)
                    v.tensor_tensor(parts[:, 2, :], parts[:, 2, :], parts[:, 3, :], ALU.add)
                    v.drain()
                    v.tensor_copy(slot_i[:, ds(e, 1), :].rearrange("p e s -> p (e s)"), slot_f[:, :])
                    v.tensor_tensor(slot_w[:, ds(e, 1), :].rearrange("p e s -> p (e s)"), parts[:, 2, :], parts[:, 4, :],
                                    ALU.add)
                    v.drain().then_inc(sems["slots_ok"], 1)
                c.leave(E // 2)

            def weighted(n, p):
                e = n * 2 + p
                v.wait_ge(sems[f"ew_in{p}"], (n + 1) * 64)
                v.wait_ge(sems["y_free"], e + 1)
                full(3)
                w = slot_w[:, ds(e, 1), :].rearrange("p e s -> p (e s)")
                v.tensor_tensor(y[p][:, :, :], ps[3][:, :].rearrange("p (s d) -> p s d", d=D),
                                eb2[p][:, :].unsqueeze(1).to_broadcast([P, CT, D]), ALU.add).then_inc(sems["free3"], 1)
                v.drain()
                v.sem_inc(sems["ew_used"], 1)
                v.tensor_tensor(y[p][:, :, :], y[p][:, :, :], w.unsqueeze(2).to_broadcast([P, CT, D]), ALU.mult)\
                    .then_inc(sems["y_ok"], 1)

            with v.Fori(0, E // 2) as n:
                c.enter(n, 0, {"full3": 2})
                for p in range(2):
                    weighted(n, p)
                c.leave(E // 2)


_INS = ['x', 'L0_tok_w1', 'L0_tok_b1', 'L0_tok_w2', 'L0_tok_b2', 'L0_attn_W_qkv', 'L0_attn_W_out', 'L0_attn_b_out',
        'L0_ffn_Wr', 'L0_ffn_W1', 'L0_ffn_b1', 'L0_ffn_W2', 'L0_ffn_b2']
_OUT = ((16, 256, 128), 'float32')


def spectrum_bases(patch=200):
    k, n = np.arange(patch // 2 + 1), np.arange(patch // 2 + 1)
    angle = 2.0 * np.pi * ((n[:, None] * k[None, :]) % patch) / patch
    cosines, sines = np.cos(angle), -np.sin(angle)
    sines[:, 0] = 0.0
    sines[:, -1] = 0.0
    return cosines.astype(np.float32), sines[1:-1].astype(np.float32)


def build(nc, shapes):
    args = [nc.dram_tensor(f"in_{n}_dram", shape, dt, kind="ExternalInput").ap() for n, shape, dt in shapes]
    cosines, sines = spectrum_bases()
    cos_c = nc.dram_tensor("cosines", cosines.shape, mybir.dt.float32, kind="ExternalInput").ap()
    sin_c = nc.dram_tensor("sines", sines.shape, mybir.dt.float32, kind="ExternalInput").ap()
    out = nc.dram_tensor("out_0_dram", _OUT[0], mybir.dt.float32, kind="ExternalOutput").ap()
    audio_tower(nc, *args, cos_c, sin_c, out)


def kernel(**inputs):
    import numpy as _np
    import concourse.bacc as _bacc
    from concourse import mybir as _mybir
    from concourse.bass_utils import run_bass_kernel_spmd as _run

    nc = _bacc.Bacc("TRN2", target_bir_lowering=False, num_devices=1)
    cosines, sines = spectrum_bases()
    arrays, shapes = {"cosines": cosines, "sines": sines}, []
    for name in _INS:
        a = _np.ascontiguousarray(inputs[name])
        arrays[f"in_{name}_dram"] = a
        shapes.append((name, a.shape, _mybir.dt.from_np(a.dtype)))
    build(nc, shapes)
    r = _run(nc, [arrays], core_ids=[0])
    return r.results[0]["out_0_dram"]
```

```python
import math
from contextlib import ExitStack

import numpy as np
import concourse.bass as bass
from concourse import mybir

ds = bass.ds


class Tally:

    def __init__(self, sem):
        self.sem, self.base, self.k = sem, 0, 0

    def up(self, n=1):
        self.k += n
        return self.base + self.k

    def now(self):
        return self.base + self.k

    def enter(self, i, start, per):
        self.start, self.per, self.outer = start, per, self.base + self.k
        self.base, self.k = self.outer + (i - start) * per, 0

    def leave(self, trips):
        assert self.k == self.per, (self.k, self.per)
        self.base, self.k = self.outer + trips * self.per, 0


class Counts:

    def __init__(self, sems):
        self.t = {n: Tally(s) for n, s in sems.items()}

    def up(self, name, n=1):
        return self.t[name].up(n)

    def job(self, s):
        return s, self.t[f"slot{s}"].up()

    def enter(self, i, start, per):
        self.loop = per
        for n, k in per.items():
            self.t[n].enter(i, start, k)

    def leave(self, trips):
        for n in self.loop:
            self.t[n].leave(trips)


PLAN = [("hid", 0), ("hid", 1), ("score", 4), ("score", 5), ("turn", 0), ("turn", 1), ("hid", 2), ("mix", 0),
        ("mix", 1), ("out", 1), ("hid", 3),
        ("score", 6), ("score", 7), ("turn", 2), ("turn", 3), ("emb", 0), ("mix", 2), ("mix", 3), ("col2", 0),
        ("turn", 4), ("turn", 5), ("col1", 0), ("mix", 4), ("mix", 5), ("qk", 0), ("qk", 1), ("qk", 2), ("qk", 3),
        ("v", 0), ("v", 1), ("next", 0), ("next", 1), ("out", 0), ("logit", 0),
        ("turn", 6), ("turn", 7), ("next", 2), ("next", 3), ("mix", 6), ("mix", 7)]
BEFORE = ("hid", "emb", "col1", "qk", "v", "next")
AFTER = (("out", 1), ("col2", 0), ("logit", 0))
START = [(k, n) for k in BEFORE for n in range({"hid": 4, "qk": 4, "v": 2, "next": 4}.get(k, 1))]
END = [("out", 1), ("col2", 0), ("logit", 0)]


def walk(c, plan, skip=()):
    at = 0
    for kind, n in plan:
        job = None
        if kind != "mix":
            if kind not in skip and (kind, n) not in skip:
                job = c.job(at % 3)
            at += 1
        elif n % 4 == 0:
            c.heads = c.job(3)
        if kind not in skip and (kind, n) not in skip:
            yield kind, n, job


def per_round(rounds):
    n = {f"slot{s}": 0 for s in range(4)}
    at = 0
    for kind, k in PLAN:
        if kind != "mix":
            n[f"slot{at % 3}"] += rounds
            at += 1
        elif k % 4 == 0:
            n["slot3"] += rounds
    return n


def audio_tower(nc, x, tok_w1, tok_b1, tok_w2, tok_b2, w_qkv, w_out, b_out, w_r, e_w1, e_b1, e_w2, e_b2,
                cos_c, sin_c, out):
    f32, bf16, i32 = mybir.dt.float32, mybir.dt.bfloat16, mybir.dt.int32
    ALU, ACT, AX = mybir.AluOpType, mybir.ActivationFunctionType, mybir.AxisListType
    RMAX, RADD = bass.bass_isa.ReduceOp.max, bass.bass_isa.ReduceOp.add

    P = 128
    B, CH, T = x.shape
    PATCH = 200
    S = -(-T // PATCH)
    BINS = PATCH // 2 + 1
    HALF = PATCH // 2
    HID = tok_w1.shape[1]
    D = tok_w2.shape[1]
    MT = 7
    MW = -(-HID // MT)
    MS = [min(MW, HID - MW * m) for m in range(MT)]
    ROWS = B * CH
    XT = ROWS // P
    NTOK = ROWS * S
    NT = NTOK // P
    G = NTOK // 512
    SEQ = NTOK // B
    HEADS, DH = 8, 64
    INNER = HEADS * DH
    E = w_r.shape[1]
    F = e_w1.shape[2]
    CAP = min(1024, NTOK)
    CT = CAP // P
    EPS = 1e-5
    TINY = 1e-36
    SIGN, PI_BITS = -2147483648, 0x40490FDB
    LOWEST = -3.0e38

    rows2 = nc.dram_tensor("rows2", (NTOK, D), f32, kind="Internal").ap()

    ctx = ExitStack()
    with ctx:
        def sb(name, shape, dt=f32):
            return ctx.enter_context(nc.sbuf_tensor(name, shape, dt))

        def carve(name, words):
            area = sb(name, [P, words])

            def stage():
                at = [0]

                def cut(shape, dt=f32):
                    n = math.prod(shape[1:]) * (1 if dt != bf16 else 0.5)
                    lo = at[0]
                    at[0] += int(n)
                    assert at[0] <= words, (name, at[0])
                    v = area[0:shape[0], lo:at[0]]
                    if dt != f32:
                        v = v.bitcast(dt)
                    if len(shape) == 2:
                        return v
                    if len(shape) == 3:
                        return v.rearrange("p (a b) -> p a b", b=shape[2])
                    return v.rearrange("p (a b c) -> p a b c", b=shape[2], c=shape[3])
                return cut
            return stage

        front = carve("front", 23552)
        back = carve("back", 3 * NTOK)
        cut = front()
        x_cur = cut([P, 2, S * PATCH])
        even = cut([P, 2 * S, BINS])
        odd = cut([P, 2 * S, HALF - 1])
        even_t = cut([BINS, 1024])
        odd_t = cut([HALF - 1, 1024])
        re = cut([BINS, 1024])
        im = cut([BINS, 1024])
        re_sq = cut([BINS, 1024])
        im_sq = cut([BINS, 1024])
        mag_sq = cut([BINS, 1024])
        den = cut([BINS, 1024])
        cosb = cut([BINS, BINS])
        sinb = cut([HALF - 1, BINS])
        cut = back()
        f_mag = cut([BINS, NTOK])
        f_ang = cut([BINS, NTOK])
        f_cor = cut([BINS, NTOK])
        w1m = sb("w1m", [BINS, HID])
        w1a = sb("w1a", [BINS, HID])
        b1c = sb("b1c", [MW, MT])
        w2t = sb("w2t", [MW, MT, D])
        b2b = sb("b2b", [P, D])
        bob = sb("bob", [P, D])
        wqkv = sb("wqkv", [P, 3 * INNER])
        wo = sb("wo", [P, INNER // P, D])
        wr = sb("wr", [P, E])
        h = sb("h", [P, NT, D])
        hid = sb("hid", [MW, MT, 512])
        stats = sb("stats", [P, 4, 6])
        mv = sb("mv", [P, 4, 2])
        var_eps = sb("var_eps", [P, 4])
        rstd = sb("rstd", [P, 4])
        zero = sb("zero", [P, 1])
        minus_half = sb("minus_half", [P, 4])
        xn = sb("xn", [P, 4, D])
        xn2 = sb("xn2", [P, 4, D])
        cut = front()
        qk = [cut([P, 8, 512]) for i in range(2)]
        v_sb = [cut([P, 4, INNER]) for i in range(2)]
        NS = 4
        sc = [cut([P, 4, SEQ]) for i in range(NS)]
        prob = [cut([P, 4, SEQ]) for i in range(NS)]
        prob_t = [cut([P, 4, SEQ]) for i in range(2)]
        o_t = cut([P, 4, SEQ])
        cut = back()
        cut([P, 2 * NTOK])
        sc2 = cut([P, 8, SEQ])
        x2_t = cut([P, 512])
        xcur = sb("xcur", [P, 512])
        top = sb("top", [P, 8, 16])
        csum = sb("csum", [P, 8, 16])
        cand = sb("cand", [P, 8, 16])
        tau = sb("tau", [P, 2, 8])
        above = sb("above", [P, 8])
        more = sb("more", [P, 2, 3])
        more_all = sb("more_all", [P, 2, 3], i32)
        seg16 = sb("seg16", [P, 8, 16])
        inv16 = sb("inv16", [P, 8, 16])
        r_sum = sb("r_sum", [P, 4])
        r_cnt = sb("r_cnt", [P, 4])
        go_w = sb("go_w", [P, 32])
        go_t = sb("go_t", [P, 32])
        go_4 = sb("go_4", [P, 4])
        go = sb("go", [P, 1], i32)
        ident = sb("ident", [P, P])
        lg = sb("lg", [P, E, NT])
        c8 = [sb(f"c8_{i}", [P, E]) for i in range(8)]
        BITS = 30
        thr = sb("thr", [P, E], i32)
        thr_c = sb("thr_c", [P, 3, E], i32)
        step_i = sb("step_i", [P, 3, E], i32)
        step_f = sb("step_f", [P, E])
        met = sb("met", [P, 3, E])
        n_met = sb("n_met", [P, E])
        keep_b = sb("keep_b", [P, E], i32)
        c24 = sb("c24", [P, 3, E])
        ones = sb("ones", [P, P])
        before = sb("before", [P, P])
        cut = front()
        pr = cut([P, E, NT])
        seg32 = cut([P, E, NT])
        sel = cut([P, E, NT])
        half16 = cut([P, E, NT], bf16)
        gt = cut([P, E, NT])
        eq = cut([P, E, NT])
        tmp = cut([P, E, NT])
        tot = cut([P, E, NT])
        rank = cut([P, E, NT])
        rank_i = cut([P, E, NT], i32)
        lo_i = cut([P, E, NT], i32)
        hi_i = cut([P, E, NT], i32)
        lo_f = cut([P, E, NT])
        hi_f = cut([P, E, NT])
        iota_r = sb("iota_r", [P, P])
        iota_p = sb("iota_p", [P, 1])
        tmp3 = cut([P, 3, E * NT])
        vals = cut([P, E, NT, 5])
        lo_hot = cut([P, NT, P], bf16)
        hi_hot = cut([P, NT, CT])
        hi_val = cut([P, NT, 5, CT], bf16)
        parts = sb("parts", [P, 5, CT])
        slot_f = sb("slot_f", [P, CT])
        slot_w = sb("slot_w", [P, E, CT])
        slot_i = sb("slot_i", [P, E, CT], i32)
        cut = back()
        ew1 = [cut([P, F]) for i in range(2)]
        ew2 = [cut([P, F // P, D]) for i in range(2)]
        eb1 = [cut([P, F // P]) for i in range(2)]
        eb2 = [cut([P, D]) for i in range(2)]
        idx = [cut([P, CT], i32) for i in range(4)]
        xg = [cut([P, CT, D]) for i in range(2)]
        xg_t = cut([P, CAP])
        eh = cut([P, F // P, CAP])
        y = [cut([P, CT, D]) for i in range(2)]

        ps = [ctx.enter_context(nc.psum_tensor(f"ps{i}", [P, 1024], f32)) for i in range(4)]

        names = ["slot0", "slot1", "slot2", "slot3",
                 "full0", "full1", "full2", "full3",
                 "free0", "free1", "free2", "free3",
                 "x_in", "tok_w_in", "att_w_in", "const", "fold", "fold_used", "re_ok", "im_ok", "sq_ok", "msq_ok",
                 "mag_ok", "den_ok", "ratio_ok", "atan_ok", "feat_ok", "ve_ok", "rstd_ok", "xn_ok",
                 "xn2_ok", "relu_ok", "more_ok", "more_seen", "held", "anymore_ok", "rows_out",
                 "mx_in", "mx_ok", "ex_in", "ex_ok", "sm_in", "sm_ok", "cnt_in", "rk_in", "hot_ok",
                 "slots_ok", "ew_in0", "ew_in1", "xg_in0", "xg_in1", "xg_used", "y_ok", "y_out", "y_free", "ew_used"]
        sems = {n: None if n.startswith("slot") and n[4:].isdigit() else ctx.enter_context(nc.semaphore(n))
                for n in names}
        block = ctx.enter_context(nc.Block())

        def layernorm(v, c, tiles, to):
            v.drain()
            for j in range(4):
                v.bn_stats(stats[:, j, :], tiles[:, j, :])
            v.drain()
            for j in range(4):
                v.bn_aggr(mv[:, j, :], stats[:, j, :])
            v.drain()
            v.tensor_scalar(var_eps[:, :], mv[:, :, 1], EPS, None, ALU.add).then_inc(sems["ve_ok"], 1)
            v.wait_ge(sems["rstd_ok"], c.up("rstd_ok"))
            for j in range(4):
                last = v.tensor_scalar(to[:, j, :], tiles[:, j, :], mv[:, j, 0:1], rstd[:, j:j + 1],
                                       ALU.subtract, ALU.mult)
            return last

        @block.sync
        def _(sp):
            c = Counts(sems)
            for n in ("free0", "free1", "free2", "free3", "fold_used", "ratio_ok", "rows_out"):
                sp.sem_inc(sems[n], 1)
            xr = x.rearrange("b c t -> (b c) t")
            with sp.Fori(0, NTOK // 1024) as i:
                sp.wait_ge(sems["fold_used"], i + 1)
                sp.dma_start(x_cur[:, :, 0:T], xr[ds(i * (2 * P), 2 * P), :].rearrange("(t p) n -> p t n", p=P))\
                    .then_inc(sems["x_in"], 16)
            with sp.Fori(0, G) as t:
                c.enter(t, 0, {"xn2_ok": 1})
                sp.wait_ge(sems["xn2_ok"], c.up("xn2_ok"))
                sp.dma_start(rows2[ds(t * 512, 512), :].rearrange("(j p) d -> p j d", p=P),
                             xn2[:, :, :]).then_inc(sems["rows_out"], 16)
                c.leave(G)
            sp.dma_start(out.rearrange("b s d -> (b s) d").rearrange("(j p) d -> p j d", p=P),
                         h[:, :, :]).then_inc(sems["rows_out"], 16)
            with sp.Fori(0, E // 2) as n:
                for p in range(2):
                    e = n * 2
                    sp.wait_ge(sems["ew_used"], e + (p + 1))
                    sp.dma_start(ew1[p][:, :], e_w1[ds(e + p, 1), :, :].rearrange("e d f -> (e d) f"))\
                        .then_inc(sems[f"ew_in{p}"], 16)
                    sp.dma_start(ew2[p][:, :, :], e_w2[ds(e + p, 1), :, :].rearrange("e (k f) d -> f (e k) d", f=P))\
                        .then_inc(sems[f"ew_in{p}"], 16)
                    sp.dma_start(eb1[p][:, :], e_b1[ds(e + p, 1), :].rearrange("e (k f) -> f (e k)", f=P),
                                 allow_slow_non_contiguous=True).then_inc(sems[f"ew_in{p}"], 16)
                    sp.dma_start(eb2[p][:, :], e_b2[ds(e + p, 1), :].partition_broadcast(P))\
                        .then_inc(sems[f"ew_in{p}"], 16)
            sp.wait_ge(sems["y_out"], 16 * E * CT)

        @block.gpsimd
        def _(g):
            c = Counts(sems)
            g.memset(ident[:, :], 0.0)
            g.memset(ones[:, :], 1.0)
            g.memset(before[:, :], 1.0)
            g.memset(minus_half[:, :], -0.5)
            g.memset(seg16[:, :, :], 1.0)
            g.iota(iota_r[:, :], [[1, P]], base=0, channel_multiplier=0, allow_small_or_imprecise_dtypes=True)
            g.iota(iota_p[:, :], [[0, 1]], base=0, channel_multiplier=1, allow_small_or_imprecise_dtypes=True)
            g.drain()
            g.affine_select(out=ident[:, :], in_=ident[:, :], compare_op=ALU.not_equal, fill=1.0,
                            base=0, pattern=[[-1, P]], channel_multiplier=1)
            g.affine_select(out=before[:, :], in_=before[:, :], compare_op=ALU.is_gt, fill=0.0,
                            base=0, pattern=[[1, P]], channel_multiplier=-1)
            g.memset(seg16[:, :, 0:1], 0.0)
            for n in range(16):
                g.memset(inv16[:, :, n:n + 1], 1.0 / (n + 1))
            g.drain()
            g.engine_nop().then_inc(sems["const"], 1)

            def power():
                g.wait_ge(sems["ve_ok"], c.up("ve_ok"))
                g.tensor_tensor(rstd[:, :], var_eps[:, :], minus_half[:, :], ALU.pow)\
                    .then_inc(sems["rstd_ok"], 1)

            def anymore(d):
                g.wait_ge(sems["more_ok"], c.up("more_ok"))
                g.sem_inc(sems["more_seen"], 1)
                g.partition_all_reduce(more_all[:, d % 2, :], more[:, d % 2, :], P, RMAX)\
                    .then_inc(sems["anymore_ok"], 1)

            def attention_round(first=False, last=False):
                anymore(1)
                if not first:
                    power()
                anymore(2)
                if not last:
                    power()
                anymore(3)
                if not last:
                    anymore(0)

            with g.Fori(0, NTOK // 1024) as i:
                g.wait_ge(sems["re_ok"], i + 1)
                g.tensor_tensor(re_sq[:, :], re[:, :], re[:, :], ALU.mult)
                g.wait_ge(sems["im_ok"], i + 1)
                g.tensor_tensor(im_sq[:, :], im[:, :], im[:, :], ALU.mult)
                g.drain()
                g.engine_nop().then_inc(sems["sq_ok"], 1)
                g.wait_ge(sems["den_ok"], i + 1)
                g.tensor_tensor(f_ang[:, ds(i * 1024, 1024)], im[:, :], den[:, :], ALU.mult)\
                    .then_inc(sems["ratio_ok"], 1)
            power()
            anymore(0)
            attention_round(first=True)
            with g.Fori(0, (G - 2) // 2) as r:
                c.enter(r, 0, {"ve_ok": 4, "more_ok": 8})
                for _ in range(2):
                    attention_round()
                c.leave((G - 2) // 2)
            attention_round(last=True)
            power()
            g.wait_ge(sems["mx_in"], 1)
            g.partition_all_reduce(c8[1][:, :], c8[0][:, :], P, RMAX).then_inc(sems["mx_ok"], 1)
            g.wait_ge(sems["sm_in"], 1)
            g.partition_all_reduce(c8[3][:, :], c8[2][:, :], P, RADD).then_inc(sems["sm_ok"], 1)
            g.wait_ge(sems["rows_out"], 16 * (G + 1) + 1)
            orow = out.rearrange("b s d -> (b s) d")

            def gather(e, p):
                g.wait_ge(sems["slots_ok"], e + 1)
                g.wait_ge(sems["xg_used"], e + 1)
                g.tensor_copy(idx[p][:, :], slot_i[:, ds(e, 1), :].rearrange("p e s -> p (e s)"))
                g.drain()
                for s in range(CT):
                    g.indirect_dma_start(xg[p][:, s, :], None, rows2[:, :],
                                         bass.IndirectOffsetOnAxis(ap=idx[p][:, s:s + 1], axis=0))\
                        .then_inc(sems[f"xg_in{p}"], 16)

            def scatter(e, p, first=False):
                g.wait_ge(sems["y_ok"], e + 1)
                if not first:
                    g.wait_ge(sems["y_out"], e * (16 * CT))
                g.sem_inc(sems["y_free"], 1)
                g.tensor_copy(idx[2 + p][:, :], slot_i[:, ds(e, 1), :].rearrange("p e s -> p (e s)"))
                g.drain()
                for s in range(CT):
                    g.indirect_dma_start(orow[:, :], bass.IndirectOffsetOnAxis(ap=idx[2 + p][:, s:s + 1], axis=0),
                                         y[p][:, s, :], None, compute_op=ALU.add)\
                        .then_inc(sems["y_out"], 16)

            g.sem_inc(sems["y_free"], 1)
            gather(0, 0)
            gather(1, 1)
            scatter(0, 0, first=True)
            with g.Fori(0, E // 2 - 1) as n:
                for p in range(2):
                    gather(n * 2 + (2 + p), p)
                    scatter(n * 2 + (1 + p), 1 - p)
            scatter(E - 1, 1)

        @block.scalar
        def _(a):
            c = Counts(sems)
            a.dma_start(cosb[:, :], cos_c).then_inc(sems["tok_w_in"], 16)
            a.dma_start(sinb[:, :], sin_c).then_inc(sems["tok_w_in"], 16)
            a.dma_start(w1m[:, :], tok_w1[0:BINS, :]).then_inc(sems["tok_w_in"], 16)
            a.dma_start(w1a[:, :], tok_w1[BINS:2 * BINS, :]).then_inc(sems["tok_w_in"], 16)
            for m in range(MT):
                a.dma_start(w2t[0:MS[m], m, :], tok_w2[m * MW:m * MW + MS[m], :]).then_inc(sems["tok_w_in"], 16)
                a.dma_start(b1c[0:MS[m], m:m + 1], tok_b1[m * MW:m * MW + MS[m]].rearrange("(p a) -> p a", a=1))\
                    .then_inc(sems["tok_w_in"], 16)
            a.dma_start(b2b[:, :], tok_b2.partition_broadcast(P)).then_inc(sems["tok_w_in"], 16)
            a.dma_start(bob[:, :], b_out.partition_broadcast(P)).then_inc(sems["tok_w_in"], 16)
            a.dma_start(wqkv[:, :], w_qkv).then_inc(sems["att_w_in"], 16)
            a.dma_start(wo[:, :, :], w_out.rearrange("(k p) d -> p k d", p=P)).then_inc(sems["att_w_in"], 16)
            a.dma_start(wr[:, :], w_r).then_inc(sems["att_w_in"], 16)

            def filled(job):
                a.wait_ge(sems[f"full{job[0]}"], job[1])

            def empty(job, dst, cols, func=ACT.Copy, **kw):
                filled(job)
                s = job[0]
                a.activation(dst, ps[s][:, 0:cols], func, **kw).then_inc(sems[f"free{s}"], 1)

            with a.Fori(0, NTOK // 1024) as i:
                c.enter(i, 0, {f"slot{s}": 1 for s in range(4)} | {"msq_ok": 1})
                jobs = [c.job(s) for s in range(4)]
                for s, (k, dst) in enumerate(((BINS, even_t), (HALF - 1, odd_t))):
                    filled(jobs[s])
                    for t in range(2):
                        last = a.activation(
                            dst[:, t * 512:(t + 1) * 512].rearrange("k (r s) -> k s r", s=S),
                            ps[s][0:k, t * 512:(t + 1) * 512].rearrange("k (s r) -> k s r", s=S), ACT.Copy)
                    last.then_inc(sems[f"free{s}"], 1)
                filled(jobs[2])
                a.wait_ge(sems["ratio_ok"], i + 1)
                a.activation(re[:, :], ps[2][0:BINS, :], ACT.Copy).then_inc(sems["free2"], 1)
                a.drain().then_inc(sems["re_ok"], 1)
                a.wait_ge(sems["msq_ok"], c.up("msq_ok"))
                a.activation(f_mag[:, ds(i * 1024, 1024)], mag_sq[:, :], ACT.Sqrt).then_inc(sems["mag_ok"], 1)
                c.leave(NTOK // 1024)
            a.wait_ge(sems["ratio_ok"], NTOK // 1024 + 1)
            with a.Fori(0, G) as t:
                a.activation(f_ang[:, ds(t * 512, 512)], f_ang[:, ds(t * 512, 512)], ACT.Arctan)\
                    .then_inc(sems["atan_ok"], 1)
            a.wait_ge(sems["tok_w_in"], 16 * (6 + 2 * MT))

            def attention_round(t, p, plan=PLAN, skip=()):
                for kind, n, job in walk(c, plan, skip):
                    if kind == "hid":
                        filled(job)
                        for m in range(2 * n, min(2 * n + 2, MT)):
                            last = a.activation(hid[0:MS[m], m, :], ps[job[0]][0:MS[m], m % 2 * 512:(m % 2 + 1) * 512],
                                                ACT.Gelu, bias=b1c[0:MS[m], m:m + 1])
                        last.then_inc(sems[f"free{job[0]}"], 1)
                    elif kind == "col1":
                        empty(job, xcur[:, :], 512)
                    elif kind == "col2":
                        empty(job, x2_t[:, :], 512)
                    elif kind == "qk":
                        empty(job, qk[1 - p][:, 2 * n:2 * n + 2, :].rearrange("p a n -> p (a n)"), 1024,
                              scale=DH ** -0.5 if n < 2 else 1.0)
                    elif kind == "v":
                        empty(job, v_sb[1 - p][:, 2 * n:2 * n + 2, :].rearrange("p a n -> p (a n)"), 1024)
                    elif kind in ("score", "next"):
                        g = (t + 1) * 8 + n if kind == "next" else t * 8 + n
                        if not (type(g) is int and g < NS):
                            a.wait_ge(sems["relu_ok"], g - (NS - 1))
                        empty(job, sc[n % NS][:, :, :].rearrange("p a n -> p (a n)"), 1024)
                    elif kind == "turn":
                        empty(job, prob_t[n % 2][:, :, :].rearrange("p a n -> p (a n)"), 1024)
                    elif kind == "mix" and n % 4 == 3:
                        empty(c.heads, o_t[:, :, :].rearrange("p a n -> p (a n)"), 1024)

            attention_round(-1, 1, START)
            attention_round(0, 0, skip=AFTER)
            with a.Fori(0, (G - 2) // 2) as r:
                c.enter(r, 0, per_round(2))
                attention_round(r * 2 + 1, 1)
                attention_round(r * 2 + 2, 0)
                c.leave((G - 2) // 2)
            attention_round(G - 1, 1, skip=BEFORE)
            attention_round(G, 0, END)

            a.wait_ge(sems["ex_in"], 1)
            a.activation(pr[:, :, :], lg[:, :, :], ACT.Exp).then_inc(sems["ex_ok"], 1)
            c.up("slot0", BITS // 2 + 3)

            def expert_columns():
                empty(c.job(2), xg_t[:, :], 1024)

            def expert_gelus(n, p):
                a.wait_ge(sems[f"ew_in{p}"], (n + 1) * 64)
                for m in range(F // P):
                    empty(c.job(m % 2), eh[:, m, :], 1024, ACT.Gelu, bias=eb1[p][:, m:m + 1])

            c.up("slot3", 2)
            expert_columns()
            with a.Fori(0, E // 2 - 1) as n:
                c.enter(n, 0, {"slot0": 4, "slot1": 4, "slot2": 2, "slot3": 4})
                for p in range(2):
                    expert_gelus(n, p)
                    expert_columns()
                c.up("slot3", 4)
                c.leave(E // 2 - 1)
            expert_gelus(E // 2 - 1, 0)
            expert_columns()
            expert_gelus(E // 2 - 1, 1)

        @block.tensor
        def _(t_):
            c = Counts(sems)
            mm = nc.tensor.matmul

            def slot(job):
                t_.wait_ge(sems[f"free{job[0]}"], job[1])
                return ps[job[0]]

            def emptied(job):
                t_.wait_ge(sems[f"free{job[0]}"], job[1] + 1)

            def done(job, ins):
                ins.then_inc(sems[f"full{job[0]}"], 1)

            t_.sem_inc(sems["xg_used"], 2)
            t_.wait_ge(sems["const"], 1)
            t_.wait_ge(sems["tok_w_in"], 16 * (6 + 2 * MT))
            t_.wait_ge(sems["att_w_in"], 48)
            with t_.Fori(0, NTOK // 1024) as i:
                c.enter(i, 0, {"fold": 2} | {f"slot{s}": 1 for s in range(4)})
                jobs = [c.job(s) for s in range(4)]
                for s, (src, k) in enumerate(((even, BINS), (odd, HALF - 1))):
                    t_.wait_ge(sems["fold"], c.up("fold"))
                    o = slot(jobs[s])
                    for q in range(2 * S):
                        last = nc.tensor.transpose(o[0:k, q * P:(q + 1) * P], src[:, q, :], ident[:, :])
                    done(jobs[s], last)
                for s, basis, cols in ((2, cosb, even_t), (3, sinb, odd_t)):
                    emptied(jobs[s - 2])
                    o = slot(jobs[s])
                    for q in range(2):
                        last = mm(o[0:BINS, q * 512:(q + 1) * 512], basis[:, :], cols[:, q * 512:(q + 1) * 512],
                                  start=True, stop=True)
                    done(jobs[s], last)
                c.leave(NTOK // 1024)

            def attention_round(t, p, plan=PLAN, skip=()):
                gelus, qkv, turned, heads = [], [], {}, {1: (3, c.t["slot3"].now())}
                for kind, n, job in walk(c, plan, skip):
                    if kind == "hid":
                        if n == 0:
                            t_.wait_ge(sems["feat_ok"], t + 2)
                        o = slot(job)
                        gelus.append(job)
                        for m in range(2 * n, min(2 * n + 2, MT)):
                            for w, f in ((w1m, f_mag), (w1a, f_ang)):
                                last = mm(o[0:MS[m], m % 2 * 512:(m % 2 + 1) * 512], w[:, m * MW:m * MW + MS[m]],
                                          f[:, ds((t + 1) * 512, 512)], start=(w is w1m), stop=(w is w1a))
                        done(job, last)
                    elif kind == "emb":
                        o = slot(job)
                        for g in gelus:
                            emptied(g)
                        for j in range(4):
                            for m in range(MT):
                                last = mm(o[:, j * D:(j + 1) * D], hid[0:MS[m], m, j * P:(j + 1) * P],
                                          w2t[0:MS[m], m, :], start=(m == 0), stop=(m == MT - 1))
                        done(job, last)
                    elif kind in ("col1", "col2"):
                        src, ok, g = (xn, "xn_ok", t + 2) if kind == "col1" else (xn2, "xn2_ok", t)
                        t_.wait_ge(sems[ok], g)
                        o = slot(job)
                        for j in range(4):
                            last = nc.tensor.transpose(o[:, j * P:(j + 1) * P], src[:, j, :], ident[:, :])
                        done(job, last)
                        if kind == "col1":
                            columns = job
                        else:
                            columns2 = job
                    elif kind == "qk":
                        if n == 0:
                            emptied(columns)
                        o = slot(job)
                        for q in range(2):
                            m = 2 * n + q
                            last = mm(o[:, q * 512:(q + 1) * 512], wqkv[:, m * P:(m + 1) * P], xcur[:, :],
                                      start=True, stop=True)
                        done(job, last)
                        qkv.append(job)
                    elif kind == "v":
                        o = slot(job)
                        for q in range(2):
                            last = mm(o[:, q * 512:(q + 1) * 512], xcur[:, (2 * n + q) * P:(2 * n + q + 1) * P],
                                      wqkv[:, 2 * INNER:3 * INNER], start=True, stop=True)
                        done(job, last)
                        qkv.append(job)
                    elif kind in ("score", "next"):
                        if kind == "next" and n == 0:
                            for g in qkv:
                                emptied(g)
                        b, hp = divmod(n, 4)
                        z = qk[1 - p if kind == "next" else p]
                        o = slot(job)
                        for it in range(2):
                            for a_ in range(2):
                                r = slice(a_ * DH, (a_ + 1) * DH)
                                last = mm(o[:, a_ * 512 + it * SEQ:a_ * 512 + (it + 1) * SEQ],
                                          z[r, hp, b * SEQ + it * P:b * SEQ + (it + 1) * P],
                                          z[r, 4 + hp, b * SEQ:(b + 1) * SEQ], start=True, stop=True)
                        done(job, last)
                    elif kind == "turn":
                        t_.wait_ge(sems["relu_ok"], t * 8 + (n + 1))
                        o = slot(job)
                        for a_ in range(2):
                            for jb in range(2):
                                for it in range(2):
                                    last = nc.tensor.transpose(
                                        o[:, a_ * 512 + jb * SEQ + it * P:a_ * 512 + jb * SEQ + (it + 1) * P],
                                        prob[n % NS][:, 2 * a_ + it, jb * P:(jb + 1) * P], ident[:, :])
                        done(job, last)
                        turned[n] = job
                    elif kind == "mix":
                        b, hp = divmod(n, 4)
                        if hp == 0:
                            slot(c.heads)
                        if n == 0:
                            heads[0] = c.heads
                        emptied(turned[n])
                        o = ps[3]
                        for jb in range(2):
                            for a_ in range(2):
                                hd = 2 * hp + a_
                                last = mm(o[a_ * DH:(a_ + 1) * DH, hp * SEQ:(hp + 1) * SEQ],
                                          v_sb[p][:, 2 * b + jb, hd * DH:(hd + 1) * DH],
                                          prob_t[n % 2][:, 2 * a_ + jb, :], start=(jb == 0), stop=(jb == 1))
                        if hp == 3:
                            done(c.heads, last)
                    elif kind == "out":
                        emptied(heads[n])
                        o = slot(job)
                        for it in range(2):
                            for k in range(4):
                                last = mm(o[:, it * D:(it + 1) * D], o_t[:, k, it * P:(it + 1) * P], wo[:, k, :],
                                          start=(k == 0), stop=(k == 3))
                        done(job, last)
                    elif kind == "logit":
                        emptied(columns2)
                        o = slot(job)
                        for j in range(4):
                            last = mm(o[:, j * E:(j + 1) * E], x2_t[:, j * P:(j + 1) * P], wr[:, :],
                                      start=True, stop=True)
                        done(job, last)

            attention_round(-1, 1, START)
            attention_round(0, 0, skip=AFTER)
            with t_.Fori(0, (G - 2) // 2) as r:
                c.enter(r, 0, per_round(2))
                attention_round(r * 2 + 1, 1)
                attention_round(r * 2 + 2, 0)
                c.leave((G - 2) // 2)
            attention_round(G - 1, 1, skip=BEFORE)
            attention_round(G, 0, END)

            def total(n, ins, cols):
                t_.wait_ge(sems["cnt_in"], n + 1)
                job = c.job(0)
                done(job, mm(slot(job)[:, 0:cols], ones[:, :], ins, start=True, stop=True))

            with t_.Fori(0, BITS // 2) as n:
                c.enter(n, 0, {"slot0": 1})
                total(n, c24[:, :, :].rearrange("p k e -> p (k e)"), 3 * E)
                c.leave(BITS // 2)
            total(BITS // 2, c8[4][:, :], E)
            for n, m in enumerate((eq, sel)):
                t_.wait_ge(sems["rk_in"], n + 1)
                job = c.job(0)
                o = slot(job)
                mm(o[:, 0:E * NT], before[:, :], m[:, :, :].rearrange("p e j -> p (e j)"), start=True, stop=True)
                done(job, mm(o[:, 512:512 + E * NT], ones[:, :], m[:, :, :].rearrange("p e j -> p (e j)"),
                             start=True, stop=True))

            def expert_slots(e):
                t_.wait_ge(sems["hot_ok"], e + 1)
                job = c.job(3)
                o = slot(job)
                for j in range(NT):
                    last = mm(o[:, 0:5 * CT], lo_hot[:, j, :], hi_val[:, j, :, :].rearrange("p v s -> p (v s)"),
                              start=(j == 0), stop=(j == NT - 1))
                done(job, last)

            def expert_columns(n, p):
                t_.wait_ge(sems[f"xg_in{p}"], (n + 1) * (16 * CT))
                job = c.job(2)
                o = slot(job)
                for s in range(CT):
                    last = nc.tensor.transpose(o[:, s * P:(s + 1) * P], xg[p][:, s, :], ident[:, :])
                done(job, last)
                return job

            def expert_hidden(n, p):
                t_.wait_ge(sems[f"ew_in{p}"], (n + 1) * 64)
                emptied((2, c.t["slot2"].now()))
                t_.sem_inc(sems["xg_used"], 1)
                jobs = []
                for m in range(F // P):
                    jobs.append(c.job(m % 2))
                    o = slot(jobs[-1])
                    for q in range(CAP // 512):
                        last = mm(o[:, q * 512:(q + 1) * 512], ew1[p][:, m * P:(m + 1) * P],
                                  xg_t[:, q * 512:(q + 1) * 512], start=True, stop=True)
                    done(jobs[-1], last)
                return jobs

            def expert_out(p, hidden):
                for job in hidden:
                    emptied(job)
                job = c.job(3)
                o = slot(job)
                for s in range(CT):
                    for k in range(F // P):
                        last = mm(o[:, s * D:(s + 1) * D], eh[:, k, s * P:(s + 1) * P], ew2[p][:, k, :],
                                  start=(k == 0), stop=(k == F // P - 1))
                done(job, last)

            expert_slots(0)
            expert_slots(1)
            expert_columns(0, 0)
            with t_.Fori(0, E // 2 - 1) as n:
                c.enter(n, 0, {"slot0": 4, "slot1": 4, "slot2": 2, "slot3": 4})
                for p in range(2):
                    hidden = expert_hidden(n, p)
                    expert_slots(n * 2 + (2 + p))
                    expert_columns(n + p, 1 - p)
                    expert_out(p, hidden)
                c.leave(E // 2 - 1)
            hidden = expert_hidden(E // 2 - 1, 0)
            expert_columns(E // 2 - 1, 1)
            expert_out(0, hidden)
            expert_out(1, expert_hidden(E // 2 - 1, 1))

        @block.vector
        def _(v):
            c = Counts(sems)

            def filled(job):
                v.wait_ge(sems[f"full{job[0]}"], job[1])
                return ps[job[0]]

            def emptied(job):
                v.wait_ge(sems[f"free{job[0]}"], job[1] + 1)

            def free(job, ins):
                ins.then_inc(sems[f"free{job[0]}"], 1)

            v.sem_inc(sems["ew_used"], 2)
            v.wait_ge(sems["const"], 1)
            v.memset(x_cur[:, :, T:S * PATCH], 0.0)
            v.memset(go_w[:, :], 0.0)
            v.memset(zero[:, :], 0.0)
            v.drain()

            def fold(i):
                xv = x_cur[:, :, :].rearrange("p t (s n) -> p (t s) n", n=PATCH)
                v.wait_ge(sems["x_in"], (i + 1) * 16)
                v.tensor_copy(even[:, :, 0:BINS:HALF], xv[:, :, 0:BINS:HALF])
                v.tensor_tensor(even[:, :, 1:HALF], xv[:, :, 1:HALF], xv[:, :, PATCH - 1:HALF:-1], ALU.add)\
                    .then_inc(sems["fold"], 1)
                v.tensor_tensor(odd[:, :, :], xv[:, :, 1:HALF], xv[:, :, PATCH - 1:HALF:-1], ALU.subtract)\
                    .then_inc(sems["fold"], 1)
                v.drain().then_inc(sems["fold_used"], 1)

            def phases(i, more):
                jobs = [c.job(s) for s in range(4)]
                o = filled(jobs[3])
                free(jobs[3], v.tensor_scalar(im[:, :], o[0:BINS, :], 0.0, None, ALU.add))
                v.drain().then_inc(sems["im_ok"], 1)
                v.tensor_scalar(den[:, :].bitcast(i32), im[:, :].bitcast(i32), SIGN, PI_BITS,
                                ALU.bitwise_and, ALU.bitwise_or)
                v.drain()
                v.wait_ge(sems["re_ok"], c.up("re_ok"))
                v.scalar_tensor_tensor(f_cor[:, ds(i * 1024, 1024)], re[:, :], 0.0, den[:, :], ALU.is_lt, ALU.mult)
                if more:
                    fold(i + 1)
                v.wait_ge(sems["sq_ok"], c.up("sq_ok"))
                v.scalar_tensor_tensor(mag_sq[:, :], re_sq[:, :], TINY, im_sq[:, :], ALU.add, ALU.add)\
                    .then_inc(sems["msq_ok"], 1)
                v.wait_ge(sems["mag_ok"], c.up("mag_ok"))
                fm = f_mag[:, ds(i * 1024, 1024)]
                v.scalar_tensor_tensor(den[:, :].bitcast(i32), re[:, :].bitcast(i32), SIGN, fm.bitcast(i32),
                                       ALU.bitwise_and, ALU.bitwise_or)
                v.drain()
                v.tensor_tensor(den[:, :], den[:, :], re[:, :], ALU.add)
                v.drain()
                v.reciprocal(den[:, :], den[:, :]).then_inc(sems["den_ok"], 1)
                v.wait_ge(sems["ratio_ok"], i + 2)
                v.sem_inc(sems["held"], 1)
                v.drain()

            fold(0)
            with v.Fori(0, NTOK // 1024 - 1) as i:
                c.enter(i, 0, {f"slot{s}": 1 for s in range(4)} | {"re_ok": 1, "sq_ok": 1, "mag_ok": 1})
                phases(i, True)
                c.leave(NTOK // 1024 - 1)
            phases(NTOK // 1024 - 1, False)
            with v.Fori(0, G) as t:
                v.wait_ge(sems["atan_ok"], t + 1)
                fa = f_ang[:, ds(t * 512, 512)]
                v.scalar_tensor_tensor(fa, fa, 2.0, f_cor[:, ds(t * 512, 512)], ALU.mult, ALU.add)\
                    .then_inc(sems["feat_ok"], 1)
            v.wait_ge(sems["tok_w_in"], 16 * (6 + 2 * MT))

            def largest(d, jobs):
                for u in range(2):
                    emptied(jobs[u])
                v.sem_inc(sems["held"], 1)
                v.drain()
                for r in range(8):
                    v.max(top[:, r, 0:8], sc[(2 * d + r // 4) % NS][:, r % 4, :])

            def largest16(d):
                v.drain()
                for r in range(8):
                    v.match_replace(sc2[:, r, :], top[:, r, 0:8], sc[(2 * d + r // 4) % NS][:, r % 4, :], LOWEST)
                v.drain()
                for r in range(8):
                    v.max(top[:, r, 8:16], sc2[:, r, :])
                v.drain()

            def thresholds(d):
                q = d % 2
                v.tensor_tensor_scan(csum[:, :, :].rearrange("p r n -> p (r n)"),
                                     seg16[:, :, :].rearrange("p r n -> p (r n)"),
                                     top[:, :, :].rearrange("p r n -> p (r n)"), 0.0, ALU.mult, ALU.add)
                v.drain()
                v.scalar_tensor_tensor(cand[:, :, :], csum[:, :, :], -1.0, inv16[:, :, :], ALU.add, ALU.mult)
                v.drain()
                v.tensor_reduce(tau[:, q, :], cand[:, :, :], AX.X, ALU.max)
                v.drain()
                v.tensor_tensor(above[:, :], top[:, :, 15], tau[:, q, :], ALU.is_gt)
                v.drain()
                v.tensor_reduce(more[:, q, 0:2], above[:, :].rearrange("p (u r) -> p u r", r=4), AX.X, ALU.max)
                v.tensor_reduce(more[:, q, 2:3], above[:, :], AX.X, ALU.max)
                v.drain().then_inc(sems["more_ok"], 1)

            def newton(d, u):
                z, ta = sc[(2 * d + u) % NS], tau[:, d % 2, 4 * u:4 * u + 4]
                for r in range(4):
                    v.scalar_tensor_tensor(sc2[:, r, :], z[:, r, :], ta[:, r:r + 1], zero[:, :].to_broadcast([P, SEQ]),
                                           ALU.subtract, ALU.max, accum_out=r_sum[:, r:r + 1])
                    v.tensor_scalar(sc2[:, 4 + r, :], z[:, r, :], ta[:, r:r + 1], None, ALU.is_gt, ALU.add,
                                    accum_out=r_cnt[:, r:r + 1])
                v.drain()
                v.tensor_scalar(r_sum[:, :], r_sum[:, :], -1.0, None, ALU.add)
                v.tensor_scalar(r_cnt[:, :], r_cnt[:, :], 1.0, None, ALU.max)
                v.drain()
                v.reciprocal(r_cnt[:, :], r_cnt[:, :])
                v.tensor_reduce(go_w[:, 0:1], r_sum[:, :], AX.X, ALU.max)
                v.drain()
                v.tensor_tensor(r_cnt[:, :], r_sum[:, :], r_cnt[:, :], ALU.mult)
                v.transpose(go_t[:, :], go_w[:, :])
                v.drain()
                v.tensor_tensor(ta, ta, r_cnt[:, :], ALU.add)
                v.tensor_reduce(r_sum[:, 0:1], go_t[:, :], AX.X, ALU.max)
                v.drain()
                for k in range(4):
                    v.tensor_copy(go_4[0:1, k:k + 1], r_sum[32 * k:32 * k + 1, 0:1])
                v.drain()
                v.tensor_reduce(r_sum[0:1, 0:1], go_4[0:1, :], AX.X, ALU.max)
                v.drain()
                v.tensor_scalar(go[0:1, :], r_sum[0:1, 0:1], 3e-6, None, ALU.is_gt)
                v.drain()

            def again(d, u, depth):
                newton(d, u)
                with v.If(v.value_load(go[0:1, 0:1], min_val=0, max_val=1) > 0):
                    if depth:
                        again(d, u, depth - 1)
                    else:
                        with v.Fori(0, 24):
                            with v.If(v.value_load(go[0:1, 0:1], min_val=0, max_val=1) > 0):
                                newton(d, u)

            def probabilities(d, turns):
                q = d % 2
                v.wait_ge(sems["anymore_ok"], c.up("anymore_ok"))
                v.sem_inc(sems["held"], 1)
                with v.If(v.value_load(more_all[0:1, q, 2:3], min_val=0, max_val=1) > 0):
                    for u in range(2):
                        with v.If(v.value_load(more_all[0:1, q, u:u + 1], min_val=0, max_val=1) > 0):
                            again(d, u, 2)
                for u in range(2):
                    if turns[u] is not None:
                        filled(turns[u])
                    for r in range(4):
                        n = 2 * d + u
                        last = v.tensor_scalar(prob[n % NS][:, r, :], sc[n % NS][:, r, :],
                                               tau[:, q, 4 * u + r:4 * u + r + 1], 0.0, ALU.subtract, ALU.max)
                    v.drain().then_inc(sems["relu_ok"], 1)

            def attention_round(t, first=False, last=False):
                skip = (AFTER if first else ()) + (BEFORE if last else ())
                jobs = {(k, n): job for k, n, job in walk(c, PLAN, skip)}
                was = c.before

                def duo(d, kind="score"):
                    return [jobs[kind, 2 * d + u] for u in range(2)]

                largest(1, [was("next", 2), was("next", 3)])
                probabilities(0, [None, None] if first else [was("turn", 4), was("turn", 5)])
                largest16(1)
                thresholds(1)
                if not first:
                    residual(jobs["out", 1], t - 1, 1)
                    second_norm(t - 1)
                largest(2, duo(2))
                probabilities(1, [None, None] if first else [was("turn", 6), was("turn", 7)])
                largest16(2)
                thresholds(2)
                if not last:
                    embeddings(jobs["emb", 0], t + 1)
                largest(3, duo(3))
                probabilities(2, [jobs["turn", 0], jobs["turn", 1]])
                largest16(3)
                thresholds(3)
                probabilities(3, [jobs["turn", 2], jobs["turn", 3]])
                residual(jobs["out", 0], t, 0)
                if not first:
                    logits(jobs["logit", 0], t - 1)
                if not last:
                    largest(0, duo(0, "next"))
                    largest16(0)
                    thresholds(0)

            def residual(job, t, b):
                o = filled(job)
                tiles = h[:, ds(t * 4 + 2 * b, 2), :]
                free(job, v.tensor_tensor(tiles, tiles, o[:, 0:2 * D].rearrange("p (j d) -> p j d", d=D), ALU.add))

            def embeddings(job, t):
                tiles = h[:, ds(t * 4, 4), :]
                free(job, v.tensor_tensor(tiles, filled(job)[:, 0:512].rearrange("p (j d) -> p j d", d=D),
                                          b2b[:, :].unsqueeze(1).to_broadcast([P, 4, D]), ALU.add))
                layernorm(v, c, tiles, xn).then_inc(sems["xn_ok"], 1)
                v.drain()
                v.tensor_tensor(tiles, tiles, bob[:, :].unsqueeze(1).to_broadcast([P, 4, D]), ALU.add)

            def second_norm(t):
                v.wait_ge(sems["rows_out"], t * 16 + 1)
                v.sem_inc(sems["held"], 1)
                layernorm(v, c, h[:, ds(t * 4, 4), :], xn2).then_inc(sems["xn2_ok"], 1)

            def logits(job, t):
                free(job, v.tensor_copy(lg[:, :, ds(t * 4, 4)].rearrange("p e j -> p j e"),
                                        filled(job)[:, 0:4 * E].rearrange("p (j e) -> p j e", e=E)))

            def remember(start=False):
                now = {s: c.t[f"slot{s}"].now() for s in range(3)}
                left = {s: 0 for s in range(3)}
                after, at = {}, sum(k != "mix" for k, _ in PLAN)
                for k, n in reversed(PLAN):
                    if k != "mix":
                        at -= 1
                        after[k, n] = (at % 3, left[at % 3])
                        left[at % 3] += 1
                if start:
                    start = [k for k in START]
                    for i, kn in enumerate(start):
                        s = i % 3
                        after[kn] = (s, sum(1 for j in range(i + 1, len(start)) if j % 3 == s))
                c.before = lambda k, n: (after[k, n][0], now[after[k, n][0]] - after[k, n][1])

            jobs = {(k, n): job for k, n, job in walk(c, START)}
            embeddings(jobs["emb", 0], 0)
            largest(0, [jobs["next", 0], jobs["next", 1]])
            largest16(0)
            thresholds(0)
            remember(start=True)
            attention_round(0, first=True)
            with v.Fori(0, (G - 2) // 2) as r:
                c.enter(r, 0, per_round(2) | {"rstd_ok": 4, "anymore_ok": 8})
                remember()
                attention_round(r * 2 + 1)
                remember()
                attention_round(r * 2 + 2)
                c.leave((G - 2) // 2)
            remember()
            attention_round(G - 1, last=True)
            jobs = {(k, n): job for k, n, job in walk(c, END)}
            residual(jobs["out", 1], G - 1, 1)
            second_norm(G - 1)
            logits(jobs["logit", 0], G - 1)

            def over_tokens(m):
                return m[:, :].unsqueeze(2).to_broadcast([P, E, NT])

            def flat(m):
                return m[:, :, :].rearrange("p e j -> p (e j)")

            v.drain()
            v.tensor_reduce(c8[0][:, :], lg[:, :, :], AX.X, ALU.max).then_inc(sems["mx_in"], 1)
            v.wait_ge(sems["mx_ok"], 1)
            v.tensor_tensor(lg[:, :, :], lg[:, :, :], over_tokens(c8[1]), ALU.subtract).then_inc(sems["ex_in"], 1)
            v.wait_ge(sems["ex_ok"], 1)
            v.tensor_reduce(c8[2][:, :], pr[:, :, :], AX.X, ALU.add).then_inc(sems["sm_in"], 1)
            v.wait_ge(sems["sm_ok"], 1)
            v.reciprocal(c8[3][:, :], c8[3][:, :])
            v.memset(thr[:, :], 0)
            v.memset(seg32[:, :, 1:NT], 1.0)
            v.memset(seg32[:, :, 0:1], 0.0)
            for k in range(3):
                v.memset(step_i[:, k, :], (k + 1) << (BITS - 2))
            v.memset(step_f[:, :], float(1 << (BITS - 2)))
            v.drain()
            v.tensor_tensor(pr[:, :, :], pr[:, :, :], over_tokens(c8[3]), ALU.mult)

            def counted(ins):
                ins.then_inc(sems["free0"], 1)

            with v.Fori(0, BITS // 2) as n:
                c.enter(n, 0, {"slot0": 1})
                v.drain()
                v.tensor_tensor(thr_c[:, :, :], thr[:, :].unsqueeze(1).to_broadcast([P, 3, E]), step_i[:, :, :],
                                ALU.bitwise_or)
                v.drain()
                v.tensor_tensor(tmp3[:, :, :].rearrange("p k (e j) -> p k e j", e=E),
                                pr[:, :, :].unsqueeze(1).to_broadcast([P, 3, E, NT]),
                                thr_c[:, :, :].bitcast(f32).unsqueeze(3).to_broadcast([P, 3, E, NT]), ALU.is_ge)
                v.drain()
                v.tensor_reduce(c24[:, :, :], tmp3[:, :, :].rearrange("p k (e j) -> p k e j", e=E), AX.X, ALU.add)\
                    .then_inc(sems["cnt_in"], 1)
                v.tensor_scalar(step_i[:, :, :], step_i[:, :, :], 2, None, ALU.logical_shift_right)
                o = filled(c.job(0))
                counted(v.tensor_scalar(met[:, :, :], o[:, 0:3 * E].rearrange("p (k e) -> p k e", e=E), float(CAP), None,
                                        ALU.is_ge))
                v.drain()
                v.tensor_reduce(n_met[:, :], met[:, :, :].rearrange("p k e -> p e k"), AX.X, ALU.add)
                v.drain()
                v.tensor_tensor(keep_b[:, :], n_met[:, :], step_f[:, :], ALU.mult)
                v.drain()
                v.tensor_tensor(thr[:, :], thr[:, :], keep_b[:, :], ALU.bitwise_or)
                v.tensor_scalar(step_f[:, :], step_f[:, :], 0.25, None, ALU.mult)
                c.leave(BITS // 2)
            v.drain()
            thr_b = thr[:, :].bitcast(f32).unsqueeze(2).to_broadcast([P, E, NT])
            v.tensor_tensor(gt[:, :, :], pr[:, :, :], thr_b, ALU.is_gt)
            v.tensor_tensor(eq[:, :, :], pr[:, :, :], thr_b, ALU.is_equal)
            v.drain()
            v.tensor_reduce(c8[4][:, :], gt[:, :, :], AX.X, ALU.add).then_inc(sems["cnt_in"], 1)
            filled(c.job(0))
            v.tensor_scalar(c8[5][:, :], ps[0][:, 0:E], -1.0, float(CAP), ALU.mult, ALU.add).then_inc(sems["free0"], 1)

            def ranks(mask):
                v.drain().then_inc(sems["rk_in"], 1)
                filled(c.job(0))
                v.tensor_copy(flat(tot), ps[0][:, 512:512 + E * NT])
                v.drain()
                v.tensor_tensor_scan(flat(rank), flat(seg32), flat(tot), 0.0, ALU.mult, ALU.add)
                v.drain()
                v.tensor_tensor(flat(rank), flat(rank), flat(tot), ALU.subtract)
                v.drain()
                v.tensor_tensor(flat(rank), flat(rank), ps[0][:, 0:E * NT], ALU.add).then_inc(sems["free0"], 1)
                v.drain()

            ranks(eq)
            v.tensor_tensor(tmp[:, :, :], rank[:, :, :], over_tokens(c8[5]), ALU.is_lt)
            v.drain()
            v.tensor_tensor(eq[:, :, :], eq[:, :, :], tmp[:, :, :], ALU.mult)
            v.drain()
            v.tensor_tensor(sel[:, :, :], eq[:, :, :], gt[:, :, :], ALU.add)
            ranks(sel)
            v.tensor_copy(rank_i[:, :, :], rank[:, :, :])
            v.drain()
            v.tensor_scalar(lo_i[:, :, :], rank_i[:, :, :], P - 1, None, ALU.bitwise_and)
            v.tensor_scalar(hi_i[:, :, :], rank_i[:, :, :], int(math.log2(P)), None, ALU.logical_shift_right)
            v.drain()
            v.tensor_copy(lo_f[:, :, :], lo_i[:, :, :])
            v.tensor_copy(hi_f[:, :, :], hi_i[:, :, :])
            v.tensor_copy(vals[:, :, :, 0], iota_r[:, 0:NT].unsqueeze(1).to_broadcast([P, E, NT]))
            v.tensor_copy(vals[:, :, :, 1], iota_p[:, :].unsqueeze(1).to_broadcast([P, E, NT]))
            v.tensor_copy(half16[:, :, :], pr[:, :, :])
            v.drain()
            v.tensor_copy(vals[:, :, :, 2], half16[:, :, :])
            v.drain()
            v.tensor_tensor(tmp[:, :, :], pr[:, :, :], vals[:, :, :, 2], ALU.subtract)
            v.drain()
            v.tensor_copy(half16[:, :, :], tmp[:, :, :])
            v.drain()
            v.tensor_copy(vals[:, :, :, 3], half16[:, :, :])
            v.drain()
            v.tensor_tensor(vals[:, :, :, 4], tmp[:, :, :], vals[:, :, :, 3], ALU.subtract)
            v.drain()

            def one_hots(e):
                lo = lo_f[:, ds(e, 1), :].rearrange("p e j -> p (e j)")
                hi = hi_f[:, ds(e, 1), :].rearrange("p e j -> p (e j)")
                on = sel[:, ds(e, 1), :].rearrange("p e j -> p (e j)")
                va = vals[:, ds(e, 1), :, :].rearrange("p e j n -> p (e j) n")
                v.tensor_tensor(lo_hot[:, :, :], iota_r[:, :].unsqueeze(1).to_broadcast([P, NT, P]),
                                lo.unsqueeze(2).to_broadcast([P, NT, P]), ALU.is_equal)
                v.tensor_tensor(hi_hot[:, :, :], iota_r[:, 0:CT].unsqueeze(1).to_broadcast([P, NT, CT]),
                                hi.unsqueeze(2).to_broadcast([P, NT, CT]), ALU.is_equal)
                v.drain()
                v.tensor_tensor(hi_hot[:, :, :], hi_hot[:, :, :], on.unsqueeze(2).to_broadcast([P, NT, CT]), ALU.mult)
                v.drain()
                for n in range(5):
                    v.tensor_tensor(hi_val[:, :, n, :], hi_hot[:, :, :],
                                    va[:, :, n].unsqueeze(2).to_broadcast([P, NT, CT]), ALU.mult)
                v.drain().then_inc(sems["hot_ok"], 1)

            def slots(e):
                one_hots(e)
                job = c.job(3)
                free(job, v.tensor_copy(parts[:, :, :].rearrange("p v s -> p (v s)"), filled(job)[:, 0:5 * CT]))
                v.drain()
                v.scalar_tensor_tensor(slot_f[:, :], parts[:, 0, :], float(P), parts[:, 1, :], ALU.mult, ALU.add)
                v.tensor_tensor(parts[:, 2, :], parts[:, 2, :], parts[:, 3, :], ALU.add)
                v.drain()
                v.tensor_copy(slot_i[:, ds(e, 1), :].rearrange("p e s -> p (e s)"), slot_f[:, :])
                v.tensor_tensor(slot_w[:, ds(e, 1), :].rearrange("p e s -> p (e s)"), parts[:, 2, :], parts[:, 4, :],
                                ALU.add)
                v.drain().then_inc(sems["slots_ok"], 1)

            def weighted(n, p):
                e = n * 2 + p
                v.wait_ge(sems[f"ew_in{p}"], (n + 1) * 64)
                v.wait_ge(sems["y_free"], e + 1)
                job = c.job(3)
                o = filled(job)
                w = slot_w[:, ds(e, 1), :].rearrange("p e s -> p (e s)")
                free(job, v.tensor_tensor(y[p][:, :, :], o[:, :].rearrange("p (s d) -> p s d", d=D),
                                          eb2[p][:, :].unsqueeze(1).to_broadcast([P, CT, D]), ALU.add))
                v.drain()
                v.sem_inc(sems["ew_used"], 1)
                v.tensor_tensor(y[p][:, :, :], y[p][:, :, :], w.unsqueeze(2).to_broadcast([P, CT, D]), ALU.mult)\
                    .then_inc(sems["y_ok"], 1)

            slots(0)
            slots(1)
            with v.Fori(0, E // 2 - 1) as n:
                c.enter(n, 0, {"slot3": 4})
                for p in range(2):
                    slots(n * 2 + (2 + p))
                    weighted(n, p)
                c.leave(E // 2 - 1)
            for p in range(2):
                weighted(E // 2 - 1, p)


_INS = ['x', 'L0_tok_w1', 'L0_tok_b1', 'L0_tok_w2', 'L0_tok_b2', 'L0_attn_W_qkv', 'L0_attn_W_out', 'L0_attn_b_out',
        'L0_ffn_Wr', 'L0_ffn_W1', 'L0_ffn_b1', 'L0_ffn_W2', 'L0_ffn_b2']
_OUT = ((16, 256, 128), 'float32')


def spectrum_bases(patch=200):
    k, n = np.arange(patch // 2 + 1), np.arange(patch // 2 + 1)
    angle = 2.0 * np.pi * ((n[:, None] * k[None, :]) % patch) / patch
    cosines, sines = np.cos(angle), -np.sin(angle)
    sines[:, 0] = 0.0
    sines[:, -1] = 0.0
    return cosines.astype(np.float32), sines[1:-1].astype(np.float32)


def build(nc, shapes):
    args = [nc.dram_tensor(f"in_{n}_dram", shape, dt, kind="ExternalInput").ap() for n, shape, dt in shapes]
    cosines, sines = spectrum_bases()
    cos_c = nc.dram_tensor("cosines", cosines.shape, mybir.dt.float32, kind="ExternalInput").ap()
    sin_c = nc.dram_tensor("sines", sines.shape, mybir.dt.float32, kind="ExternalInput").ap()
    out = nc.dram_tensor("out_0_dram", _OUT[0], mybir.dt.float32, kind="ExternalOutput").ap()
    audio_tower(nc, *args, cos_c, sin_c, out)


def kernel(**inputs):
    import numpy as _np
    import concourse.bacc as _bacc
    from concourse import mybir as _mybir
    from concourse.bass_utils import run_bass_kernel_spmd as _run

    nc = _bacc.Bacc("TRN2", target_bir_lowering=False, num_devices=1)
    cosines, sines = spectrum_bases()
    arrays, shapes = {"cosines": cosines, "sines": sines}, []
    for name in _INS:
        a = _np.ascontiguousarray(inputs[name])
        arrays[f"in_{name}_dram"] = a
        shapes.append((name, a.shape, _mybir.dt.from_np(a.dtype)))
    build(nc, shapes)
    r = _run(nc, [arrays], core_ids=[0])
    return r.results[0]["out_0_dram"]
```

```python
import math
from contextlib import ExitStack

import numpy as np
import concourse.bass as bass
from concourse import mybir

ds = bass.ds


class Tally:

    def __init__(self, sem):
        self.sem, self.base, self.k = sem, 0, 0

    def up(self, n=1):
        self.k += n
        return self.base + self.k

    def now(self):
        return self.base + self.k

    def enter(self, i, start, per):
        self.start, self.per, self.outer = start, per, self.base + self.k
        self.base, self.k = self.outer + (i - start) * per, 0

    def leave(self, trips):
        assert self.k == self.per, (self.k, self.per)
        self.base, self.k = self.outer + trips * self.per, 0


class Counts:

    def __init__(self, sems):
        self.t = {n: Tally(s) for n, s in sems.items()}

    def up(self, name, n=1):
        return self.t[name].up(n)

    def job(self, s):
        return s, self.t[f"slot{s}"].up()

    def enter(self, i, start, per):
        self.loop = per
        for n, k in per.items():
            self.t[n].enter(i, start, k)

    def leave(self, trips):
        for n in self.loop:
            self.t[n].leave(trips)


PLAN = [("score", 4), ("turn", 0), ("out", 1), ("turn", 1), ("relu", 2), ("score", 5), ("mix", 0),
        ("mix", 1), ("col1", 0), ("turn", 2), ("qk", 0), ("qk", 1), ("relu", 3), ("qk", 2), ("qk", 3),
        ("turn", 3), ("score", 6), ("score", 7), ("mix", 2), ("v", 0), ("v", 1), ("mix", 3), ("relu", 4),
        ("hid", 0), ("relu", 5), ("hid", 1), ("next", 0), ("turn", 4), ("next", 1), ("turn", 5), ("next", 2),
        ("mix", 4), ("next", 3), ("out", 0), ("col2", 0), ("mix", 5), ("relu", 6), ("relu", 7), ("logit", 0),
        ("hid", 2), ("turn", 6), ("hid", 3), ("turn", 7), ("relu next", 0), ("mix", 6), ("mix", 7),
        ("relu next", 1), ("emb", 1)]
NO_JOB = ("mix", "relu", "relu next", "magnitudes", "half phases")
BEFORE = ("hid", "emb", "col1", "qk", "v", "next", "relu next")
AFTER = (("out", 1), ("col2", 0), ("logit", 0))
START = [("first", 0), ("first", 3), ("first", 2), ("first", 1), ("magnitudes", 3), ("emb", 0), ("col1", 0),
         ("qk", 0), ("qk", 1), ("qk", 2), ("qk", 3), ("next", 0), ("next", 2), ("next", 1), ("hid", 0),
         ("v", 1), ("half phases", 2), ("half phases", 3), ("v", 0), ("next", 3), ("relu next", 0),
         ("hid", 1), ("relu next", 1), ("hid", 2), ("hid", 3), ("emb", 1)]
END = [("out", 1), ("col2", 0), ("logit", 0)]

STEPS = [("residual", 1), ("second norm", 0), ("largest", 2), ("thresholds", 2), ("settle", 2),
         ("largest", 3), ("thresholds", 3), ("settle", 3), ("largest", 0), ("thresholds", 0),
         ("residual", 0), ("largest", 1), ("settle", 0), ("thresholds", 1), ("settle", 1), ("embeddings", 0),
         ("first norm", 0)]
STEPS_BEFORE = tuple((s, d) for s in ("largest", "thresholds", "settle") for d in (0, 1))
STEPS_AFTER = (("residual", 1), "second norm")


def steps(skip=()):
    return [(step, n) for step, n in STEPS
            if not (skip and (AFTER[0] in skip and (step in STEPS_AFTER or (step, n) in STEPS_AFTER)
                              or "next" in skip and (step, n) in STEPS_BEFORE
                              or "emb" in skip and step in ("embeddings", "first norm")))]


def walk(c, plan, skip=()):
    at = 0
    for kind, n in plan:
        job = None
        if kind not in NO_JOB:
            if kind not in skip and (kind, n) not in skip:
                job = c.job(at % 3)
            at += 1
        elif kind == "mix" and n % 4 == 0:
            c.heads = c.job(3)
        if kind not in skip and (kind, n) not in skip:
            yield kind, n, job


def per_round(rounds):
    n = {f"slot{s}": 0 for s in range(4)}
    at = 0
    for kind, k in PLAN:
        if kind not in NO_JOB:
            n[f"slot{at % 3}"] += rounds
            at += 1
        elif kind == "mix" and k % 4 == 0:
            n["slot3"] += rounds
    return n


def audio_tower(nc, x, tok_w1, tok_b1, tok_w2, tok_b2, w_qkv, w_out, b_out, w_r, e_w1, e_b1, e_w2, e_b2,
                cos_c, sin_c, out):
    f32, bf16, i32 = mybir.dt.float32, mybir.dt.bfloat16, mybir.dt.int32
    ALU, ACT, AX = mybir.AluOpType, mybir.ActivationFunctionType, mybir.AxisListType
    RMAX, RADD = bass.bass_isa.ReduceOp.max, bass.bass_isa.ReduceOp.add

    P = 128
    B, CH, T = x.shape
    PATCH = 200
    S = -(-T // PATCH)
    BINS = PATCH // 2 + 1
    HALF = PATCH // 2
    HID = tok_w1.shape[1]
    D = tok_w2.shape[1]
    MT = 7
    MW = -(-HID // MT)
    MS = [min(MW, HID - MW * m) for m in range(MT)]
    ROWS = B * CH
    PARTS = ROWS * S // 1024
    NTOK = ROWS * S
    NT = NTOK // P
    G = NTOK // 512
    SEQ = NTOK // B
    HEADS, DH = 8, 64
    INNER = HEADS * DH
    E = w_r.shape[1]
    F = e_w1.shape[2]
    CAP = min(1024, NTOK)
    CT = CAP // P
    EPS = 1e-5
    TINY = 1e-36
    SIGN, PI_BITS = -2147483648, 0x40490FDB
    LOWEST = -3.0e38

    rows2 = nc.dram_tensor("rows2", (NTOK, D), f32, kind="Internal").ap()

    ctx = ExitStack()
    with ctx:
        def sb(name, shape, dt=f32):
            return ctx.enter_context(nc.sbuf_tensor(name, shape, dt))

        def carve(name, words):
            area = sb(name, [P, words])

            def stage(start=0):
                at = [start]

                def cut(shape, dt=f32):
                    n = math.prod(shape[1:]) * (1 if dt != bf16 else 0.5)
                    lo = at[0]
                    at[0] += int(n)
                    assert at[0] <= words, (name, at[0])
                    v = area[0:shape[0], lo:at[0]]
                    if dt != f32:
                        v = v.bitcast(dt)
                    if len(shape) == 2:
                        return v
                    if len(shape) == 3:
                        return v.rearrange("p (a b) -> p a b", b=shape[2])
                    return v.rearrange("p (a b c) -> p a b c", b=shape[2], c=shape[3])
                return cut
            return stage

        front = carve("front", 23552)
        back = carve("back", 3 * NTOK)
        cut = front()
        x_cur = cut([P, 2, S * PATCH])
        even = cut([P, 2 * S, BINS])
        odd = cut([P, 2 * S, HALF - 1])
        even_t = cut([BINS, 1024])
        odd_t = cut([HALF - 1, 1024])
        re_sq = cut([BINS, 1024])
        im_sq = cut([BINS, 1024])
        cosb = cut([BINS, BINS])
        sinb = cut([HALF - 1, BINS])
        cut = front(16384)
        re = [cut([BINS, 1024]) for i in range(2)]
        im = [cut([BINS, 1024]) for i in range(2)]
        pi_im = cut([BINS, 1024])
        mag_sq = cut([BINS, 1024])
        den = cut([BINS, 1024])
        cut = back()
        f_mag = cut([BINS, NTOK])
        f_ang = cut([BINS, NTOK])
        f_cor = cut([BINS, NTOK])
        w1m = sb("w1m", [BINS, HID])
        w1a = sb("w1a", [BINS, HID])
        b1c = sb("b1c", [MW, MT])
        w2t = sb("w2t", [MW, MT, D])
        b2b = sb("b2b", [P, D])
        bob = sb("bob", [P, D])
        wqkv = sb("wqkv", [P, 3 * INNER])
        wo = sb("wo", [P, INNER // P, D])
        wr = sb("wr", [P, E])
        h = sb("h", [P, NT, D])
        hid = sb("hid", [MW, MT, 512])
        stats = sb("stats", [P, 4, 6])
        mv = sb("mv", [P, 4, 2])
        var_eps = sb("var_eps", [P, 4])
        rstd = sb("rstd", [P, 4])
        zero = sb("zero", [P, 1])
        minus_half = sb("minus_half", [P, 4])
        xn = sb("xn", [P, 4, D])
        xn2 = sb("xn2", [P, 4, D])
        cut = front()
        qk = [cut([P, 8, 512]) for i in range(2)]
        v_sb = [cut([P, 4, INNER]) for i in range(2)]
        NS = 8
        sc = [cut([P, 4, SEQ]) for i in range(NS)]
        prob = [cut([P, 4, SEQ]) for i in range(2)]
        o_t = cut([P, 4, SEQ])
        cut = back()
        cut([P, 2 * NTOK])
        sc2 = cut([P, 8, SEQ])
        prob_t = [cut([P, 4, SEQ]) for i in range(2)]
        x2_t = sb("x2_t", [P, 512])
        emb = sb("emb", [P, 512])
        att = [sb(f"att{i}", [P, 2 * D]) for i in range(2)]
        xcur = sb("xcur", [P, 512])
        top = sb("top", [P, 8, 16])
        csum = sb("csum", [P, 8, 16])
        cand = sb("cand", [P, 8, 16])
        tau = sb("tau", [P, 4, 8])
        minus_tau = sb("minus_tau", [P, 4, 8])
        above = sb("above", [P, 8])
        more = sb("more", [P, 4, 3])
        more_all = sb("more_all", [P, 4, 3], i32)
        seg16 = sb("seg16", [P, 8, 16])
        inv16 = sb("inv16", [P, 8, 16])
        r_sum = sb("r_sum", [P, 4])
        r_cnt = sb("r_cnt", [P, 4])
        go_w = sb("go_w", [P, 32])
        go_t = sb("go_t", [P, 32])
        go_4 = sb("go_4", [P, 4])
        go = sb("go", [P, 1], i32)
        ident = sb("ident", [P, P])
        lg = sb("lg", [P, E, NT])
        lg_max, all_max = sb("lg_max", [P, E]), sb("all_max", [P, E])
        ex_sum, all_sum = sb("ex_sum", [P, E]), sb("all_sum", [P, E])
        above_thr, wanted = sb("above_thr", [P, E]), sb("wanted", [P, E])
        JB = 8
        BITS = 30
        reached = sb("reached", [P, 4, E], i32)
        thr = sb("thr", [P, E], i32)
        thr_c = sb("thr_c", [P, 3, E], i32)
        step_i = sb("step_i", [P, 3, E], i32)
        c24 = sb("c24", [P, 3, E])
        ones = sb("ones", [P, P], bf16)
        not_before = sb("not_before", [P, P], bf16)
        cut = front()
        pr = cut([P, E, NT])
        seg32 = cut([P, E, NT])
        sel = cut([P, E, NT], bf16)
        gt = cut([P, E, NT], bf16)
        eq = cut([P, E, NT], bf16)
        first = cut([P, E, NT], bf16)
        half16 = cut([P, E, NT], bf16)
        rank = cut([P, E, NT])
        rank_i = cut([P, E, NT], i32)
        lo_i = cut([P, E, NT], i32)
        hi_i = cut([P, E, NT], i32)
        rest = cut([P, E, NT])
        iota_r = sb("iota_r", [P, P])
        iota_p = sb("iota_p", [P, 1])
        met = cut([P, 3 * E, NT], bf16)
        vals = cut([P, E, NT, 5])
        lo_hot = cut([P, NT, P], bf16)
        hi_hot = cut([P, NT, CT])
        hi_val = cut([P, NT, 5, CT], bf16)
        parts = cut([P, 5, CT])
        slot_f = sb("slot_f", [P, CT])
        slot_w = cut([P, E, CT])
        slot_i = cut([P, E, CT], i32)
        cut = back()
        ew1 = [cut([P, F]) for i in range(2)]
        ew2 = [cut([P, F // P, D]) for i in range(2)]
        eb1 = [cut([P, F // P]) for i in range(2)]
        eb2 = [cut([P, D]) for i in range(2)]
        gather_at = [cut([P, CT], i32) for i in range(2)]
        add_at = [cut([P, CT], i32) for i in range(2)]
        xg = [cut([P, CT, D]) for i in range(2)]
        xg_t = cut([P, CAP])
        eh = cut([P, F // P, CAP])
        y = [cut([P, CT, D]) for i in range(2)]

        ps = [ctx.enter_context(nc.psum_tensor(f"ps{i}", [P, 1024], f32)) for i in range(4)]

        names = ["slot0", "slot1", "slot2", "slot3",
                 "full0", "full1", "full2", "full3",
                 "free0", "free1", "free2", "free3",
                 "held", "pool_held",
                 "x_in", "zero_ok", "basis_in", "tok_w_in", "att_w_in", "const", "fold", "fold_used",
                 "re_ok", "im_ok", "sq_ok", "msq_ok",
                 "mag_ok", "den_ok", "ratio_ok", "atan_ok", "feat_ok", "ve_ok", "rstd_ok", "xn_ok",
                 "xn2_ok", "relu_ok", "tau_ok", "more_ok", "anymore_ok", "rows_out",
                 "mx_in", "mx_ok", "ex_in", "ex_ok", "sm_in", "sm_ok", "pr_ok", "round_ok",
                 "rest_ok", "vals_ok", "cnt_in", "rk_in", "hot_ok",
                 "slots_ok", "ew_in0", "ew_in1", "xg_in0", "xg_in1", "xg_used", "y_ok", "y_out", "y_free", "ew_used"]
        sems = {n: None if n.startswith("slot") and n[4:].isdigit() else ctx.enter_context(nc.semaphore(n))
                for n in names}
        block = ctx.enter_context(nc.Block())

        def layernorm(v, c, tiles, to):
            v.drain()
            for j in range(4):
                v.bn_stats(stats[:, j, :], tiles[:, j, :])
            v.drain()
            for j in range(4):
                v.bn_aggr(mv[:, j, :], stats[:, j, :])
            v.drain()
            v.tensor_scalar(var_eps[:, :], mv[:, :, 1], EPS, None, ALU.add).then_inc(sems["ve_ok"], 1)
            v.wait_ge(sems["rstd_ok"], c.up("rstd_ok"))
            for j in range(4):
                last = v.tensor_scalar(to[:, j, :], tiles[:, j, :], mv[:, j, 0:1], rstd[:, j:j + 1],
                                       ALU.subtract, ALU.mult)
            return last

        @block.sync
        def _(sp):
            c = Counts(sems)
            for n in ("free0", "free1", "free2", "free3", "fold_used", "rows_out"):
                sp.sem_inc(sems[n], 1)
            xr = x.rearrange("b c t -> (b c) t")
            with sp.Fori(0, NTOK // 1024) as i:
                sp.wait_ge(sems["fold_used"], i + 1)
                sp.dma_start(x_cur[:, :, 0:T], xr[ds(i * (2 * P), 2 * P), :].rearrange("(t p) n -> p t n", p=P))\
                    .then_inc(sems["x_in"], 16)
            sp.dma_start(w1m[:, :], tok_w1[0:BINS, :]).then_inc(sems["tok_w_in"], 16)
            sp.dma_start(w1a[:, :], tok_w1[BINS:2 * BINS, :]).then_inc(sems["tok_w_in"], 16)
            for m in range(MT):
                sp.dma_start(w2t[0:MS[m], m, :], tok_w2[m * MW:m * MW + MS[m], :]).then_inc(sems["tok_w_in"], 16)
                sp.dma_start(b1c[0:MS[m], m:m + 1], tok_b1[m * MW:m * MW + MS[m]].rearrange("(p a) -> p a", a=1))\
                    .then_inc(sems["tok_w_in"], 16)
            sp.dma_start(b2b[:, :], tok_b2.partition_broadcast(P)).then_inc(sems["tok_w_in"], 16)
            sp.dma_start(bob[:, :], b_out.partition_broadcast(P)).then_inc(sems["tok_w_in"], 16)
            sp.dma_start(wqkv[:, :], w_qkv).then_inc(sems["att_w_in"], 16)
            sp.dma_start(wo[:, :, :], w_out.rearrange("(k p) d -> p k d", p=P)).then_inc(sems["att_w_in"], 16)
            sp.dma_start(wr[:, :], w_r).then_inc(sems["att_w_in"], 16)
            with sp.Fori(0, G) as t:
                c.enter(t, 0, {"xn2_ok": 1})
                sp.wait_ge(sems["xn2_ok"], c.up("xn2_ok"))
                sp.dma_start(rows2[ds(t * 512, 512), :].rearrange("(j p) d -> p j d", p=P),
                             xn2[:, :, :]).then_inc(sems["rows_out"], 16)
                c.leave(G)
            sp.dma_start(out.rearrange("b s d -> (b s) d").rearrange("(j p) d -> p j d", p=P),
                         h[:, :, :]).then_inc(sems["rows_out"], 16)
            with sp.Fori(0, E // 2) as n:
                for p in range(2):
                    e = n * 2
                    sp.wait_ge(sems["ew_used"], e + (p + 1))
                    sp.dma_start(ew1[p][:, :], e_w1[ds(e + p, 1), :, :].rearrange("e d f -> (e d) f"))\
                        .then_inc(sems[f"ew_in{p}"], 16)
                    sp.dma_start(ew2[p][:, :, :], e_w2[ds(e + p, 1), :, :].rearrange("e (k f) d -> f (e k) d", f=P))\
                        .then_inc(sems[f"ew_in{p}"], 16)
                    sp.dma_start(eb1[p][:, :], e_b1[ds(e + p, 1), :].rearrange("e (k f) -> f (e k)", f=P),
                                 allow_slow_non_contiguous=True).then_inc(sems[f"ew_in{p}"], 16)
                    sp.dma_start(eb2[p][:, :], e_b2[ds(e + p, 1), :].partition_broadcast(P))\
                        .then_inc(sems[f"ew_in{p}"], 16)
            sp.wait_ge(sems["y_out"], 16 * E * CT)

        @block.gpsimd
        def _(g):
            c = Counts(sems)
            g.memset(ident[:, :], 0.0)
            g.memset(ones[:, :], 1.0)
            g.memset(not_before[:, :], 0.0)
            g.memset(minus_half[:, :], -0.5)
            g.memset(seg16[:, :, :], 1.0)
            g.iota(iota_r[:, :], [[1, P]], base=0, channel_multiplier=0, allow_small_or_imprecise_dtypes=True)
            g.iota(iota_p[:, :], [[0, 1]], base=0, channel_multiplier=1, allow_small_or_imprecise_dtypes=True)
            g.drain()
            g.affine_select(out=ident[:, :], in_=ident[:, :], compare_op=ALU.not_equal, fill=1.0,
                            base=0, pattern=[[-1, P]], channel_multiplier=1)
            g.affine_select(out=not_before[:, :], in_=not_before[:, :], compare_op=ALU.is_gt, fill=-1.0,
                            base=0, pattern=[[1, P]], channel_multiplier=-1)
            g.memset(seg16[:, :, 0:1], 0.0)
            for n in range(16):
                g.memset(inv16[:, :, n:n + 1], 1.0 / (n + 1))
            g.drain()
            g.engine_nop().then_inc(sems["const"], 1)

            def power():
                g.wait_ge(sems["ve_ok"], c.up("ve_ok"))
                g.tensor_tensor(rstd[:, :], var_eps[:, :], minus_half[:, :], ALU.pow)\
                    .then_inc(sems["rstd_ok"], 1)

            def anymore(d):
                g.wait_ge(sems["more_ok"], c.up("more_ok"))
                g.sem_inc(sems["pool_held"], 1)
                g.partition_all_reduce(more_all[:, d, :], more[:, d, :], P, RMAX)\
                    .then_inc(sems["anymore_ok"], 1)

            def attention_round(skip=()):
                for step, n in steps(skip):
                    if step in ("first norm", "second norm"):
                        power()
                    elif step == "thresholds":
                        anymore(n)

            for i in range(PARTS):
                if i + 1 == PARTS:
                    power()
                g.wait_ge(sems["den_ok"], i + 1)
                g.tensor_tensor(f_ang[:, i * 1024:(i + 1) * 1024], im[i % 2][:, :], den[:, :], ALU.mult)\
                    .then_inc(sems["ratio_ok"], 1)
            anymore(0)
            anymore(1)
            power()
            attention_round(AFTER)
            with g.Fori(0, G // 2 - 2) as r:
                c.enter(r, 0, {"ve_ok": 4, "more_ok": 8})
                for _ in range(2):
                    attention_round()
                c.leave(G // 2 - 2)
            attention_round()
            attention_round(("hid", "emb"))
            attention_round(BEFORE)
            power()
            g.wait_ge(sems["mx_in"], 1)
            g.partition_all_reduce(all_max[:, :], lg_max[:, :], P, RMAX).then_inc(sems["mx_ok"], 1)
            g.wait_ge(sems["sm_in"], 1)
            g.partition_all_reduce(all_sum[:, :], ex_sum[:, :], P, RADD).then_inc(sems["sm_ok"], 1)
            g.wait_ge(sems["ex_ok"], 1)
            g.tensor_copy(vals[:, :, :, 0], iota_r[:, 0:NT].unsqueeze(1).to_broadcast([P, E, NT]))
            g.tensor_copy(vals[:, :, :, 1], iota_p[:, :].unsqueeze(1).to_broadcast([P, E, NT]))
            g.wait_ge(sems["round_ok"], 1)
            g.tensor_tensor(rest[:, :, :], pr[:, :, :], vals[:, :, :, 2], ALU.subtract).then_inc(sems["rest_ok"], 1)
            g.wait_ge(sems["round_ok"], 2)
            g.tensor_tensor(vals[:, :, :, 4], rest[:, :, :], vals[:, :, :, 3], ALU.subtract)
            g.drain()
            g.engine_nop().then_inc(sems["vals_ok"], 1)
            g.wait_ge(sems["rows_out"], 16 * (G + 1) + 1)
            orow = out.rearrange("b s d -> (b s) d")

            def gather(e, p):
                g.wait_ge(sems["slots_ok"], e + 1)
                g.wait_ge(sems["xg_used"], e + 1)
                g.sem_inc(sems["pool_held"], 1)
                for s in range(CT):
                    g.indirect_dma_start(xg[p][:, s, :], None, rows2[:, :],
                                         bass.IndirectOffsetOnAxis(ap=gather_at[p][:, s:s + 1], axis=0))\
                        .then_inc(sems[f"xg_in{p}"], 16)

            def scatter(e, p, first=False):
                g.wait_ge(sems["y_ok"], e + 1)
                if not first:
                    g.wait_ge(sems["y_out"], e * (16 * CT))
                g.sem_inc(sems["y_free"], 1)
                for s in range(CT):
                    g.indirect_dma_start(orow[:, :], bass.IndirectOffsetOnAxis(ap=add_at[p][:, s:s + 1], axis=0),
                                         y[p][:, s, :], None, compute_op=ALU.add)\
                        .then_inc(sems["y_out"], 16)

            g.sem_inc(sems["y_free"], 1)
            gather(0, 0)
            gather(1, 1)
            gather(2, 0)
            scatter(0, 0, first=True)
            with g.Fori(0, (E - 4) // 2) as n:
                for p in range(2):
                    gather(n * 2 + (3 + p), 1 - p)
                    scatter(n * 2 + (1 + p), 1 - p)
            gather(E - 1, 1)
            scatter(E - 3, 1)
            scatter(E - 2, 0)
            scatter(E - 1, 1)

        @block.scalar
        def _(a):
            c = Counts(sems)
            a.dma_start(cosb[:, :], cos_c).then_inc(sems["basis_in"], 16)
            a.dma_start(sinb[:, :], sin_c).then_inc(sems["basis_in"], 16)

            def filled(job):
                a.wait_ge(sems[f"full{job[0]}"], job[1])

            def empty(job, dst, cols, func=ACT.Copy, **kw):
                filled(job)
                s = job[0]
                a.activation(dst, ps[s][:, 0:cols], func, **kw).then_inc(sems[f"free{s}"], 1)

            def columns(i):
                for s, (k, dst) in enumerate(((BINS, even_t), (HALF - 1, odd_t))):
                    filled(c.job(s))
                    for t in range(2):
                        last = a.activation(
                            dst[:, t * 512:(t + 1) * 512].rearrange("k (r s) -> k s r", s=S),
                            ps[s][0:k, t * 512:(t + 1) * 512].rearrange("k (s r) -> k s r", s=S), ACT.Copy)
                    last.then_inc(sems[f"free{s}"], 1)

            def real_imaginary(i):
                if i > 1:
                    a.wait_ge(sems["ratio_ok"], i - 1)
                filled(c.job(2))
                a.activation(re[i % 2][:, :], ps[2][0:BINS, :], ACT.Copy)
                a.drain().then_inc(sems["re_ok"], 1)
                filled(c.job(3))
                a.activation(im[i % 2][:, :], ps[3][0:BINS, :], ACT.Identity, bias=zero[0:BINS, :])
                a.drain().then_inc(sems["im_ok"], 1)
                a.activation(re_sq[:, :], ps[2][0:BINS, :], ACT.Square).then_inc(sems["free2"], 1)
                a.activation(im_sq[:, :], ps[3][0:BINS, :], ACT.Square).then_inc(sems["free3"], 1)
                a.drain().then_inc(sems["sq_ok"], 1)

            def magnitudes(i):
                a.wait_ge(sems["msq_ok"], i + 1)
                a.activation(f_mag[:, i * 1024:(i + 1) * 1024], mag_sq[:, :], ACT.Sqrt).then_inc(sems["mag_ok"], 1)

            def half_phases(i):
                a.wait_ge(sems["ratio_ok"], i + 1)
                for t in (2 * i, 2 * i + 1):
                    a.activation(f_ang[:, t * 512:(t + 1) * 512], f_ang[:, t * 512:(t + 1) * 512], ACT.Arctan)\
                        .then_inc(sems["atan_ok"], 1)

            a.wait_ge(sems["zero_ok"], 1)
            columns(0)
            real_imaginary(0)
            for i in range(PARTS - 1):
                columns(i + 1)
                magnitudes(i)
                real_imaginary(i + 1)
                if i:
                    half_phases(i - 1)
            a.wait_ge(sems["tok_w_in"], 16 * (4 + 2 * MT))

            def attention_round(t, p, plan=PLAN, skip=()):
                for kind, n, job in walk(c, plan, skip):
                    if kind in ("first", "hid"):
                        filled(job)
                        for m in range(2 * n, min(2 * n + 2, MT)):
                            last = a.activation(hid[0:MS[m], m, :], ps[job[0]][0:MS[m], m % 2 * 512:(m % 2 + 1) * 512],
                                                ACT.Gelu, bias=b1c[0:MS[m], m:m + 1])
                        last.then_inc(sems[f"free{job[0]}"], 1)
                    elif kind == "emb":
                        empty(job, emb[:, :], 512)
                    elif kind == "out":
                        empty(job, att[n][:, :], 2 * D)
                    elif kind == "logit":
                        filled(job)
                        a.activation(lg[:, :, ds((t - 1) * 4, 4)].rearrange("p e j -> p j e"),
                                     ps[job[0]][:, 0:4 * E].rearrange("p (j e) -> p j e", e=E), ACT.Copy)\
                            .then_inc(sems[f"free{job[0]}"], 1)
                    elif kind == "magnitudes":
                        magnitudes(n)
                    elif kind == "half phases":
                        half_phases(n)
                    elif kind == "col1":
                        empty(job, xcur[:, :], 512)
                    elif kind == "col2":
                        empty(job, x2_t[:, :], 512)
                    elif kind == "qk":
                        empty(job, qk[1 - p][:, 2 * n:2 * n + 2, :].rearrange("p a n -> p (a n)"), 1024,
                              scale=DH ** -0.5 if n < 2 else 1.0)
                    elif kind == "v":
                        empty(job, v_sb[1 - p][:, 2 * n:2 * n + 2, :].rearrange("p a n -> p (a n)"), 1024)
                    elif kind in ("score", "next"):
                        empty(job, sc[n][:, :, :].rearrange("p a n -> p (a n)"), 1024)
                    elif kind in ("relu", "relu next"):
                        a.wait_ge(sems["tau_ok"], (t + 1 if kind == "relu next" else t) * 4 + (n // 2 + 1))
                        for r in range(4):
                            a.activation(prob[n % 2][:, r, :], sc[n][:, r, :], ACT.Relu,
                                         bias=minus_tau[:, n // 2, n % 2 * 4 + r:n % 2 * 4 + r + 1])
                        a.drain().then_inc(sems["relu_ok"], 1)
                    elif kind == "turn":
                        empty(job, prob_t[n % 2][:, :, :].rearrange("p a n -> p (a n)"), 1024)
                    elif kind == "mix" and n % 4 == 3:
                        empty(c.heads, o_t[:, :, :].rearrange("p a n -> p (a n)"), 1024)

            attention_round(-1, 1, START)
            attention_round(0, 0, skip=AFTER)
            with a.Fori(0, G // 2 - 2) as r:
                c.enter(r, 0, per_round(2))
                attention_round(r * 2 + 1, 1)
                attention_round(r * 2 + 2, 0)
                c.leave(G // 2 - 2)
            attention_round(G - 3, 1)
            attention_round(G - 2, 0, skip=("hid", "emb"))
            attention_round(G - 1, 1, skip=BEFORE)
            attention_round(G, 0, END)

            a.wait_ge(sems["ex_in"], 1)
            a.activation(pr[:, :, :], lg[:, :, :], ACT.Exp).then_inc(sems["ex_ok"], 1)
            for n, (part, ok) in enumerate(((pr, "pr_ok"), (rest, "rest_ok"))):
                a.wait_ge(sems[ok], 1)
                a.activation(half16[:, :, :], part[:, :, :], ACT.Copy)
                a.drain()
                a.activation(vals[:, :, :, 2 + n], half16[:, :, :], ACT.Copy)
                a.drain().then_inc(sems["round_ok"], 1)
            c.up("slot0", BITS // 2 + 3)

            def expert_columns():
                empty(c.job(2), xg_t[:, :], 1024)

            def expert_gelus(n, p):
                a.wait_ge(sems[f"ew_in{p}"], (n + 1) * 64)
                for m in range(F // P):
                    empty(c.job(m % 2), eh[:, m, :], 1024, ACT.Gelu, bias=eb1[p][:, m:m + 1])

            c.up("slot3", 2)
            expert_columns()
            with a.Fori(0, E // 2 - 1) as n:
                c.enter(n, 0, {"slot0": 4, "slot1": 4, "slot2": 2, "slot3": 4})
                for p in range(2):
                    expert_gelus(n, p)
                    expert_columns()
                c.up("slot3", 4)
                c.leave(E // 2 - 1)
            expert_gelus(E // 2 - 1, 0)
            expert_columns()
            expert_gelus(E // 2 - 1, 1)

        @block.tensor
        def _(t_):
            c = Counts(sems)
            mm = nc.tensor.matmul

            def slot(job):
                c.hidden.pop(job[0], None)
                t_.wait_ge(sems[f"free{job[0]}"], job[1])
                return ps[job[0]]

            def emptied(job):
                t_.wait_ge(sems[f"free{job[0]}"], job[1] + 1)

            def done(job, ins):
                ins.then_inc(sems[f"full{job[0]}"], 1)

            c.hidden = {}
            t_.sem_inc(sems["xg_used"], 2)
            t_.wait_ge(sems["const"], 1)
            with t_.Fori(0, NTOK // 1024) as i:
                c.enter(i, 0, {"fold": 2} | {f"slot{s}": 1 for s in range(4)})
                jobs = [c.job(s) for s in range(4)]
                for s, (src, k) in enumerate(((even, BINS), (odd, HALF - 1))):
                    t_.wait_ge(sems["fold"], c.up("fold"))
                    o = slot(jobs[s])
                    for q in range(2 * S):
                        last = nc.tensor.transpose(o[0:k, q * P:(q + 1) * P], src[:, q, :], ident[:, :])
                    done(jobs[s], last)
                t_.wait_ge(sems["basis_in"], 32)
                for s, basis, cols in ((2, cosb, even_t), (3, sinb, odd_t)):
                    emptied(jobs[s - 2])
                    o = slot(jobs[s])
                    for q in range(2):
                        last = mm(o[0:BINS, q * 512:(q + 1) * 512], basis[:, :], cols[:, q * 512:(q + 1) * 512],
                                  start=True, stop=True)
                    done(jobs[s], last)
                c.leave(NTOK // 1024)

            def attention_round(t, p, plan=PLAN, skip=()):
                qkv, turned, heads = [], {}, {1: (3, c.t["slot3"].now())}
                for kind, n, job in walk(c, plan, skip):
                    if kind in ("first", "hid"):
                        g = t + 1 if kind == "first" else t + 2
                        if n == 0:
                            t_.wait_ge(sems["feat_ok"], g + 1)
                        o = slot(job)
                        c.hidden[job[0]] = job
                        for m in range(2 * n, min(2 * n + 2, MT)):
                            for w, f in ((w1m, f_mag), (w1a, f_ang)):
                                last = mm(o[0:MS[m], m % 2 * 512:(m % 2 + 1) * 512], w[:, m * MW:m * MW + MS[m]],
                                          f[:, ds(g * 512, 512)], start=(w is w1m), stop=(w is w1a))
                        done(job, last)
                    elif kind == "emb":
                        o = slot(job)
                        for gelu in c.hidden.values():
                            emptied(gelu)
                        c.hidden = {}
                        for j in range(4):
                            for m in range(MT):
                                last = mm(o[:, j * D:(j + 1) * D], hid[0:MS[m], m, j * P:(j + 1) * P],
                                          w2t[0:MS[m], m, :], start=(m == 0), stop=(m == MT - 1))
                        done(job, last)
                    elif kind in ("col1", "col2"):
                        src, ok, g = (xn, "xn_ok", t + 2) if kind == "col1" else (xn2, "xn2_ok", t)
                        t_.wait_ge(sems[ok], g)
                        o = slot(job)
                        for j in range(4):
                            last = nc.tensor.transpose(o[:, j * P:(j + 1) * P], src[:, j, :], ident[:, :])
                        done(job, last)
                        if kind == "col1":
                            columns = job
                        else:
                            columns2 = job
                    elif kind == "qk":
                        if n == 0:
                            emptied(columns)
                        o = slot(job)
                        for q in range(2):
                            m = 2 * n + q
                            last = mm(o[:, q * 512:(q + 1) * 512], wqkv[:, m * P:(m + 1) * P], xcur[:, :],
                                      start=True, stop=True)
                        done(job, last)
                        qkv.append(job)
                    elif kind == "v":
                        o = slot(job)
                        for q in range(2):
                            last = mm(o[:, q * 512:(q + 1) * 512], xcur[:, (2 * n + q) * P:(2 * n + q + 1) * P],
                                      wqkv[:, 2 * INNER:3 * INNER], start=True, stop=True)
                        done(job, last)
                        qkv.append(job)
                    elif kind in ("score", "next"):
                        b, hp = divmod(n, 4)
                        z = qk[1 - p if kind == "next" else p]
                        o = slot(job)
                        if kind == "next" and n == 0:
                            for g in {g[0]: g for g in qkv if g[0] != job[0]}.values():
                                emptied(g)
                        for it in range(2):
                            for a_ in range(2):
                                r = slice(a_ * DH, (a_ + 1) * DH)
                                last = mm(o[:, a_ * 512 + it * SEQ:a_ * 512 + (it + 1) * SEQ],
                                          z[r, hp, b * SEQ + it * P:b * SEQ + (it + 1) * P],
                                          z[r, 4 + hp, b * SEQ:(b + 1) * SEQ], start=True, stop=True)
                        done(job, last)
                    elif kind == "turn":
                        t_.wait_ge(sems["relu_ok"], t * 8 + (n + 1))
                        o = slot(job)
                        for a_ in range(2):
                            for jb in range(2):
                                for it in range(2):
                                    last = nc.tensor.transpose(
                                        o[:, a_ * 512 + jb * SEQ + it * P:a_ * 512 + jb * SEQ + (it + 1) * P],
                                        prob[n % 2][:, 2 * a_ + it, jb * P:(jb + 1) * P], ident[:, :])
                        done(job, last)
                        turned[n] = job
                    elif kind == "mix":
                        b, hp = divmod(n, 4)
                        if hp == 0:
                            slot(c.heads)
                        if n == 0:
                            heads[0] = c.heads
                        emptied(turned[n])
                        o = ps[3]
                        for jb in range(2):
                            for a_ in range(2):
                                hd = 2 * hp + a_
                                last = mm(o[a_ * DH:(a_ + 1) * DH, hp * SEQ:(hp + 1) * SEQ],
                                          v_sb[p][:, 2 * b + jb, hd * DH:(hd + 1) * DH],
                                          prob_t[n % 2][:, 2 * a_ + jb, :], start=(jb == 0), stop=(jb == 1))
                        if hp == 3:
                            done(c.heads, last)
                    elif kind == "out":
                        emptied(heads[n])
                        o = slot(job)
                        for it in range(2):
                            for k in range(4):
                                last = mm(o[:, it * D:(it + 1) * D], o_t[:, k, it * P:(it + 1) * P], wo[:, k, :],
                                          start=(k == 0), stop=(k == 3))
                        done(job, last)
                    elif kind == "logit":
                        emptied(columns2)
                        o = slot(job)
                        for j in range(4):
                            last = mm(o[:, j * E:(j + 1) * E], x2_t[:, j * P:(j + 1) * P], wr[:, :],
                                      start=True, stop=True)
                        done(job, last)

            t_.wait_ge(sems["tok_w_in"], 16 * (4 + 2 * MT))
            t_.wait_ge(sems["att_w_in"], 48)
            attention_round(-1, 1, START)
            attention_round(0, 0, skip=AFTER)
            with t_.Fori(0, G // 2 - 2) as r:
                c.enter(r, 0, per_round(2))
                attention_round(r * 2 + 1, 1)
                attention_round(r * 2 + 2, 0)
                c.leave(G // 2 - 2)
            attention_round(G - 3, 1)
            attention_round(G - 2, 0, skip=("hid", "emb"))
            attention_round(G - 1, 1, skip=BEFORE)
            attention_round(G, 0, END)

            def total(n, mask, rows):
                t_.wait_ge(sems["cnt_in"], n + 1)
                job = c.job(0)
                o = slot(job)[:, 0:rows * JB].rearrange("p (r j) -> p r j", j=JB)
                for j in range(0, NT, JB):
                    last = mm(o, ones[:, :], mask[:, :, j:j + JB], start=(j == 0), stop=(j + JB == NT))
                done(job, last)

            with t_.Fori(0, BITS // 10) as n:
                c.enter(n, 0, {"slot0": 5})
                for k in range(5):
                    total(n * 5 + k, met, 3 * E)
                c.leave(BITS // 10)
            total(BITS // 2, gt, E)
            for n, m in enumerate((eq, sel)):
                t_.wait_ge(sems["rk_in"], n + 1)
                job = c.job(0)
                o = slot(job)
                mm(o[:, 0:E * NT], not_before[:, :], m[:, :, :].rearrange("p e j -> p (e j)"), start=True, stop=True)
                done(job, mm(o[:, 512:512 + E * NT], ones[:, :], m[:, :, :].rearrange("p e j -> p (e j)"),
                             start=True, stop=True))

            def expert_slots(e):
                t_.wait_ge(sems["hot_ok"], e + 1)
                job = c.job(3)
                o = slot(job)
                for j in range(NT):
                    last = mm(o[:, 0:5 * CT], lo_hot[:, j, :], hi_val[:, j, :, :].rearrange("p v s -> p (v s)"),
                              start=(j == 0), stop=(j == NT - 1))
                done(job, last)

            def expert_columns(n, p):
                t_.wait_ge(sems[f"xg_in{p}"], (n + 1) * (16 * CT))
                job = c.job(2)
                o = slot(job)
                for s in range(CT):
                    last = nc.tensor.transpose(o[:, s * P:(s + 1) * P], xg[p][:, s, :], ident[:, :])
                done(job, last)
                return job

            def expert_hidden(n, p):
                t_.wait_ge(sems[f"ew_in{p}"], (n + 1) * 64)
                emptied((2, c.t["slot2"].now()))
                t_.sem_inc(sems["xg_used"], 1)
                jobs = []
                for m in range(F // P):
                    jobs.append(c.job(m % 2))
                    o = slot(jobs[-1])
                    for q in range(CAP // 512):
                        last = mm(o[:, q * 512:(q + 1) * 512], ew1[p][:, m * P:(m + 1) * P],
                                  xg_t[:, q * 512:(q + 1) * 512], start=True, stop=True)
                    done(jobs[-1], last)
                return jobs

            def expert_out(p, hidden):
                for job in hidden:
                    emptied(job)
                job = c.job(3)
                o = slot(job)
                for s in range(CT):
                    for k in range(F // P):
                        last = mm(o[:, s * D:(s + 1) * D], eh[:, k, s * P:(s + 1) * P], ew2[p][:, k, :],
                                  start=(k == 0), stop=(k == F // P - 1))
                done(job, last)

            expert_slots(0)
            expert_slots(1)
            expert_columns(0, 0)
            with t_.Fori(0, E // 2 - 1) as n:
                c.enter(n, 0, {"slot0": 4, "slot1": 4, "slot2": 2, "slot3": 4})
                for p in range(2):
                    hidden = expert_hidden(n, p)
                    expert_slots(n * 2 + (2 + p))
                    expert_columns(n + p, 1 - p)
                    expert_out(p, hidden)
                c.leave(E // 2 - 1)
            hidden = expert_hidden(E // 2 - 1, 0)
            expert_columns(E // 2 - 1, 1)
            expert_out(0, hidden)
            expert_out(1, expert_hidden(E // 2 - 1, 1))

        @block.vector
        def _(v):
            c = Counts(sems)

            def filled(job):
                v.wait_ge(sems[f"full{job[0]}"], job[1])
                return ps[job[0]]

            def emptied(job):
                v.wait_ge(sems[f"free{job[0]}"], job[1] + 1)

            def free(job, ins):
                ins.then_inc(sems[f"free{job[0]}"], 1)

            v.sem_inc(sems["ew_used"], 2)
            v.wait_ge(sems["const"], 1)
            v.memset(x_cur[:, :, T:S * PATCH], 0.0)
            v.memset(go_w[:, :], 0.0)
            v.memset(zero[:, :], 0.0)
            v.drain().then_inc(sems["zero_ok"], 1)

            def fold(i):
                xv = x_cur[:, :, :].rearrange("p t (s n) -> p (t s) n", n=PATCH)
                if i:
                    for s in range(2):
                        v.wait_ge(sems[f"full{s}"], i)
                v.wait_ge(sems["x_in"], (i + 1) * 16)
                v.tensor_copy(even[:, :, 0:BINS:HALF], xv[:, :, 0:BINS:HALF])
                v.tensor_tensor(even[:, :, 1:HALF], xv[:, :, 1:HALF], xv[:, :, PATCH - 1:HALF:-1], ALU.add)\
                    .then_inc(sems["fold"], 1)
                v.tensor_tensor(odd[:, :, :], xv[:, :, 1:HALF], xv[:, :, PATCH - 1:HALF:-1], ALU.subtract)\
                    .then_inc(sems["fold"], 1)
                v.drain().then_inc(sems["fold_used"], 1)

            def features(groups):
                for t in groups:
                    v.wait_ge(sems["atan_ok"], t + 1)
                    fa = f_ang[:, t * 512:(t + 1) * 512]
                    v.scalar_tensor_tensor(fa, fa, 2.0, f_cor[:, t * 512:(t + 1) * 512], ALU.mult, ALU.add)\
                        .then_inc(sems["feat_ok"], 1)

            def phases(i):
                part = slice(i * 1024, (i + 1) * 1024)
                r, m = re[i % 2], im[i % 2]
                for s in range(4):
                    c.job(s)
                if i > 1:
                    features(range(2 * i - 4, 2 * i - 2))
                v.wait_ge(sems["im_ok"], i + 1)
                v.tensor_scalar(pi_im[:, :].bitcast(i32), m[:, :].bitcast(i32), SIGN, PI_BITS,
                                ALU.bitwise_and, ALU.bitwise_or)
                v.drain()
                v.wait_ge(sems["re_ok"], i + 1)
                v.scalar_tensor_tensor(f_cor[:, part], r[:, :], 0.0, pi_im[:, :], ALU.is_lt, ALU.mult)
                v.wait_ge(sems["sq_ok"], i + 1)
                v.scalar_tensor_tensor(mag_sq[:, :], re_sq[:, :], TINY, im_sq[:, :], ALU.add, ALU.add)\
                    .then_inc(sems["msq_ok"], 1)
                if i + 2 < PARTS:
                    fold(i + 2)
                v.wait_ge(sems["mag_ok"], i + 1)
                if i:
                    v.wait_ge(sems["ratio_ok"], i)
                v.scalar_tensor_tensor(den[:, :].bitcast(i32), r[:, :].bitcast(i32), SIGN,
                                       f_mag[:, part].bitcast(i32), ALU.bitwise_and, ALU.bitwise_or)
                v.drain()
                v.tensor_tensor(den[:, :], den[:, :], r[:, :], ALU.add)
                if i + 1 == PARTS:
                    v.wait_ge(sems["tok_w_in"], 16 * (4 + 2 * MT))
                    c.start = {(k, n): job for k, n, job in walk(c, START)}
                    embeddings(c.start["emb", 0], 0)
                    first_norm(0)
                v.drain()
                v.reciprocal(den[:, :], den[:, :]).then_inc(sems["den_ok"], 1)


            def largest(d, jobs):
                for u in range(2):
                    emptied(jobs[u])
                v.sem_inc(sems["held"], 1)
                v.drain()
                for r in range(8):
                    v.max(top[:, r, 0:8], sc[2 * d + r // 4][:, r % 4, :])

            def thresholds(d):
                v.drain()
                for r in range(8):
                    v.match_replace(sc2[:, r, :], top[:, r, 0:8], sc[2 * d + r // 4][:, r % 4, :], LOWEST)
                v.drain()
                for r in range(8):
                    v.max(top[:, r, 8:16], sc2[:, r, :])
                v.drain()

                v.tensor_tensor_scan(csum[:, :, :].rearrange("p r n -> p (r n)"),
                                     seg16[:, :, :].rearrange("p r n -> p (r n)"),
                                     top[:, :, :].rearrange("p r n -> p (r n)"), 0.0, ALU.mult, ALU.add)
                v.drain()
                v.scalar_tensor_tensor(cand[:, :, :], csum[:, :, :], -1.0, inv16[:, :, :], ALU.add, ALU.mult)
                v.drain()
                v.tensor_reduce(tau[:, d, :], cand[:, :, :], AX.X, ALU.max)
                v.drain()
                v.tensor_tensor(above[:, :], top[:, :, 15], tau[:, d, :], ALU.is_gt)
                v.drain()
                v.tensor_reduce(more[:, d, 0:2], above[:, :].rearrange("p (u r) -> p u r", r=4), AX.X, ALU.max)
                v.tensor_reduce(more[:, d, 2:3], above[:, :], AX.X, ALU.max)
                v.drain().then_inc(sems["more_ok"], 1)

            def newton(d, u):
                z, ta = sc[2 * d + u], tau[:, d, 4 * u:4 * u + 4]
                for r in range(4):
                    v.scalar_tensor_tensor(sc2[:, r, :], z[:, r, :], ta[:, r:r + 1], zero[:, :].to_broadcast([P, SEQ]),
                                           ALU.subtract, ALU.max, accum_out=r_sum[:, r:r + 1])
                    v.tensor_scalar(sc2[:, 4 + r, :], z[:, r, :], ta[:, r:r + 1], None, ALU.is_gt, ALU.add,
                                    accum_out=r_cnt[:, r:r + 1])
                v.drain()
                v.tensor_scalar(r_sum[:, :], r_sum[:, :], -1.0, None, ALU.add)
                v.tensor_scalar(r_cnt[:, :], r_cnt[:, :], 1.0, None, ALU.max)
                v.drain()
                v.reciprocal(r_cnt[:, :], r_cnt[:, :])
                v.tensor_reduce(go_w[:, 0:1], r_sum[:, :], AX.X, ALU.max)
                v.drain()
                v.tensor_tensor(r_cnt[:, :], r_sum[:, :], r_cnt[:, :], ALU.mult)
                v.transpose(go_t[:, :], go_w[:, :])
                v.drain()
                v.tensor_tensor(ta, ta, r_cnt[:, :], ALU.add)
                v.tensor_reduce(r_sum[:, 0:1], go_t[:, :], AX.X, ALU.max)
                v.drain()
                for k in range(4):
                    v.tensor_copy(go_4[0:1, k:k + 1], r_sum[32 * k:32 * k + 1, 0:1])
                v.drain()
                v.tensor_reduce(r_sum[0:1, 0:1], go_4[0:1, :], AX.X, ALU.max)
                v.drain()
                v.tensor_scalar(go[0:1, :], r_sum[0:1, 0:1], 3e-6, None, ALU.is_gt)
                v.drain()

            def again(d, u, depth):
                newton(d, u)
                with v.If(v.value_load(go[0:1, 0:1], min_val=0, max_val=1) > 0):
                    if depth:
                        again(d, u, depth - 1)
                    else:
                        with v.Fori(0, 24):
                            with v.If(v.value_load(go[0:1, 0:1], min_val=0, max_val=1) > 0):
                                newton(d, u)

            def settle(d):
                v.wait_ge(sems["anymore_ok"], c.up("anymore_ok"))
                v.sem_inc(sems["held"], 1)
                with v.If(v.value_load(more_all[0:1, d, 2:3], min_val=0, max_val=1) > 0):
                    for u in range(2):
                        with v.If(v.value_load(more_all[0:1, d, u:u + 1], min_val=0, max_val=1) > 0):
                            again(d, u, 2)
                v.drain()
                v.tensor_scalar(minus_tau[:, d, :], tau[:, d, :], -1.0, None, ALU.mult).then_inc(sems["tau_ok"], 1)

            def attention_round(t, skip=()):
                jobs = {(k, n): job for k, n, job in walk(c, PLAN, skip)}
                for step, n in steps(skip):
                    if step == "largest":
                        kind, u = ("next", 2 * n) if n < 2 else ("score", 2 * n)
                        largest(n, [jobs[kind, u], jobs[kind, u + 1]])
                    elif step == "thresholds":
                        thresholds(n)
                    elif step == "settle":
                        settle(n)
                    elif step == "residual":
                        residual(jobs["out", n], t - n, n)
                    elif step == "second norm":
                        second_norm(t - 1)
                    elif step == "embeddings":
                        embeddings(jobs["emb", 1], t + 2)
                    elif step == "first norm":
                        first_norm(t + 2)

            def residual(job, t, b):
                emptied(job)
                tiles = h[:, ds(t * 4 + 2 * b, 2), :]
                v.tensor_tensor(tiles, tiles, att[b][:, :].rearrange("p (j d) -> p j d", d=D), ALU.add)

            def embeddings(job, t):
                tiles = h[:, ds(t * 4, 4), :]
                emptied(job)
                v.sem_inc(sems["held"], 1)
                v.tensor_tensor(tiles, emb[:, :].rearrange("p (j d) -> p j d", d=D),
                                b2b[:, :].unsqueeze(1).to_broadcast([P, 4, D]), ALU.add)

            def first_norm(t):
                tiles = h[:, ds(t * 4, 4), :]
                layernorm(v, c, tiles, xn).then_inc(sems["xn_ok"], 1)
                v.drain()
                v.tensor_tensor(tiles, tiles, bob[:, :].unsqueeze(1).to_broadcast([P, 4, D]), ALU.add)

            def second_norm(t):
                v.wait_ge(sems["rows_out"], t * 16 + 1)
                v.sem_inc(sems["held"], 1)
                layernorm(v, c, h[:, ds(t * 4, 4), :], xn2).then_inc(sems["xn2_ok"], 1)

            fold(0)
            fold(1)
            for i in range(PARTS):
                phases(i)
            jobs = c.start
            largest(0, [jobs["next", 0], jobs["next", 1]])
            thresholds(0)
            features(range(G - 4, G))
            settle(0)
            largest(1, [jobs["next", 2], jobs["next", 3]])
            thresholds(1)
            settle(1)
            embeddings(jobs["emb", 1], 1)
            first_norm(1)
            attention_round(0, AFTER)
            with v.Fori(0, G // 2 - 2) as r:
                c.enter(r, 0, per_round(2) | {"rstd_ok": 4, "anymore_ok": 8})
                attention_round(r * 2 + 1)
                attention_round(r * 2 + 2)
                c.leave(G // 2 - 2)
            attention_round(G - 3)
            attention_round(G - 2, ("hid", "emb"))
            attention_round(G - 1, BEFORE)
            jobs = {(k, n): job for k, n, job in walk(c, END)}
            residual(jobs["out", 1], G - 1, 1)
            second_norm(G - 1)
            emptied(jobs["logit", 0])

            def over_tokens(m):
                return m[:, :].unsqueeze(2).to_broadcast([P, E, NT])

            def flat(m):
                return m[:, :, :].rearrange("p e j -> p (e j)")

            v.drain()
            v.tensor_reduce(lg_max[:, :], lg[:, :, :], AX.X, ALU.max).then_inc(sems["mx_in"], 1)
            v.wait_ge(sems["mx_ok"], 1)
            v.tensor_tensor(lg[:, :, :], lg[:, :, :], over_tokens(all_max), ALU.subtract).then_inc(sems["ex_in"], 1)
            v.wait_ge(sems["ex_ok"], 1)
            v.tensor_reduce(ex_sum[:, :], pr[:, :, :], AX.X, ALU.add).then_inc(sems["sm_in"], 1)
            v.wait_ge(sems["sm_ok"], 1)
            v.reciprocal(all_sum[:, :], all_sum[:, :])
            v.memset(thr[:, :], 0)
            v.memset(seg32[:, :, 1:NT], 1.0)
            v.memset(seg32[:, :, 0:1], 0.0)
            for k in range(3):
                v.memset(step_i[:, k, :], (k + 1) << (BITS - 2))
            v.drain()
            v.tensor_tensor(pr[:, :, :], pr[:, :, :], over_tokens(all_sum), ALU.mult).then_inc(sems["pr_ok"], 1)

            def add_up(counts, rows):
                v.tensor_reduce(counts, ps[0][:, 0:rows * JB].rearrange("p (r j) -> p r j", j=JB), AX.X, ALU.add)\
                    .then_inc(sems["free0"], 1)

            def two_bits():
                v.drain()
                v.tensor_tensor(thr_c[:, :, :], thr[:, :].unsqueeze(1).to_broadcast([P, 3, E]), step_i[:, :, :],
                                ALU.bitwise_or)
                v.drain()
                v.tensor_tensor(met[:, :, :].rearrange("p (k e) j -> p k e j", e=E),
                                pr[:, :, :].unsqueeze(1).to_broadcast([P, 3, E, NT]),
                                thr_c[:, :, :].bitcast(f32).unsqueeze(3).to_broadcast([P, 3, E, NT]), ALU.is_ge)\
                    .then_inc(sems["cnt_in"], 1)
                v.tensor_copy(reached[:, 0, :], thr[:, :])
                v.tensor_scalar(step_i[:, :, :], step_i[:, :, :], 2, None, ALU.logical_shift_right)
                filled(c.job(0))
                add_up(c24[:, :, :].rearrange("p k e -> p (k e)"), 3 * E)
                v.drain()
                v.scalar_tensor_tensor(reached[:, 1:4, :].bitcast(f32), c24[:, :, :], float(CAP),
                                       thr_c[:, :, :].bitcast(f32), ALU.is_ge, ALU.mult)
                v.drain()
                v.tensor_reduce(thr[:, :].bitcast(f32), reached[:, :, :].bitcast(f32).rearrange("p k e -> p e k"),
                                AX.X, ALU.max)

            with v.Fori(0, BITS // 10) as n:
                c.enter(n, 0, {"slot0": 5})
                for _ in range(5):
                    two_bits()
                c.leave(BITS // 10)
            v.drain()
            thr_b = thr[:, :].bitcast(f32).unsqueeze(2).to_broadcast([P, E, NT])
            v.tensor_tensor(gt[:, :, :], pr[:, :, :], thr_b, ALU.is_gt)
            v.tensor_tensor(eq[:, :, :], pr[:, :, :], thr_b, ALU.is_equal)
            v.drain().then_inc(sems["cnt_in"], 1)
            filled(c.job(0))
            add_up(above_thr[:, :], E)
            v.drain()
            v.tensor_scalar(wanted[:, :], above_thr[:, :], -1.0, float(CAP), ALU.mult, ALU.add)

            def ranks(mask):
                v.drain().then_inc(sems["rk_in"], 1)
                filled(c.job(0))
                v.tensor_tensor_scan(flat(rank), flat(seg32), ps[0][:, 512:512 + E * NT], 0.0, ALU.mult, ALU.add)
                v.drain()
                v.tensor_tensor(flat(rank), flat(rank), ps[0][:, 0:E * NT], ALU.add).then_inc(sems["free0"], 1)
                v.drain()

            ranks(eq)
            v.tensor_tensor(first[:, :, :], rank[:, :, :], over_tokens(wanted), ALU.is_lt)
            v.drain()
            v.tensor_tensor(eq[:, :, :], eq[:, :, :], first[:, :, :], ALU.mult)
            v.drain()
            v.tensor_tensor(sel[:, :, :], eq[:, :, :], gt[:, :, :], ALU.add)
            ranks(sel)
            v.tensor_copy(rank_i[:, :, :], rank[:, :, :])
            v.drain()
            v.tensor_scalar(lo_i[:, :, :], rank_i[:, :, :], P - 1, None, ALU.bitwise_and)
            v.tensor_scalar(hi_i[:, :, :], rank_i[:, :, :], int(math.log2(P)), None, ALU.logical_shift_right)
            v.drain()
            v.wait_ge(sems["vals_ok"], 1)
            v.sem_inc(sems["held"], 1)

            def one_hots(e):
                lo = lo_i[:, ds(e, 1), :].rearrange("p e j -> p (e j)")
                hi = hi_i[:, ds(e, 1), :].rearrange("p e j -> p (e j)")
                on = sel[:, ds(e, 1), :].rearrange("p e j -> p (e j)")
                va = vals[:, ds(e, 1), :, :].rearrange("p e j n -> p (e j) n")
                v.tensor_tensor(lo_hot[:, :, :], iota_r[:, :].unsqueeze(1).to_broadcast([P, NT, P]),
                                lo.unsqueeze(2).to_broadcast([P, NT, P]), ALU.is_equal)
                v.tensor_tensor(hi_hot[:, :, :], iota_r[:, 0:CT].unsqueeze(1).to_broadcast([P, NT, CT]),
                                hi.unsqueeze(2).to_broadcast([P, NT, CT]), ALU.is_equal)
                v.drain()
                v.tensor_tensor(hi_hot[:, :, :], hi_hot[:, :, :], on.unsqueeze(2).to_broadcast([P, NT, CT]), ALU.mult)
                v.drain()
                for n in range(5):
                    v.tensor_tensor(hi_val[:, :, n, :], hi_hot[:, :, :],
                                    va[:, :, n].unsqueeze(2).to_broadcast([P, NT, CT]), ALU.mult)
                v.drain().then_inc(sems["hot_ok"], 1)

            def slots(n, p, first=False):
                e = n * 2 + p
                job = c.job(3)
                free(job, v.tensor_copy(parts[:, :, :].rearrange("p v s -> p (v s)"), filled(job)[:, 0:5 * CT]))
                v.drain()
                v.scalar_tensor_tensor(slot_f[:, :], parts[:, 0, :], float(P), parts[:, 1, :], ALU.mult, ALU.add)
                v.tensor_tensor(parts[:, 2, :], parts[:, 2, :], parts[:, 3, :], ALU.add)
                v.drain()
                v.tensor_copy(slot_i[:, ds(e, 1), :].rearrange("p e s -> p (e s)"), slot_f[:, :])
                if not first:
                    v.wait_ge(sems[f"xg_in{p}"], n * (16 * CT))
                v.tensor_copy(gather_at[p][:, :], slot_f[:, :])
                v.tensor_tensor(slot_w[:, ds(e, 1), :].rearrange("p e s -> p (e s)"), parts[:, 2, :], parts[:, 4, :],
                                ALU.add)
                v.drain().then_inc(sems["slots_ok"], 1)

            def weighted(n, p):
                e = n * 2 + p
                v.wait_ge(sems[f"ew_in{p}"], (n + 1) * 64)
                v.wait_ge(sems["y_free"], e + 1)
                job = c.job(3)
                o = filled(job)
                w = slot_w[:, ds(e, 1), :].rearrange("p e s -> p (e s)")
                free(job, v.tensor_tensor(y[p][:, :, :], o[:, :].rearrange("p (s d) -> p s d", d=D),
                                          eb2[p][:, :].unsqueeze(1).to_broadcast([P, CT, D]), ALU.add))
                v.tensor_copy(add_at[p][:, :], slot_i[:, ds(e, 1), :].rearrange("p e s -> p (e s)"))
                v.drain()
                v.sem_inc(sems["ew_used"], 1)
                v.tensor_tensor(y[p][:, :, :], y[p][:, :, :], w.unsqueeze(2).to_broadcast([P, CT, D]), ALU.mult)\
                    .then_inc(sems["y_ok"], 1)

            one_hots(0)
            for p in range(2):
                slots(0, p, first=True)
                one_hots(1 + p)
            with v.Fori(0, E // 2 - 2) as n:
                c.enter(n, 0, {"slot3": 4})
                for p in range(2):
                    slots(n + 1, p)
                    one_hots(n * 2 + (3 + p))
                    weighted(n, p)
                c.leave(E // 2 - 2)
            slots(E // 2 - 1, 0)
            one_hots(E - 1)
            weighted(E // 2 - 2, 0)
            slots(E // 2 - 1, 1)
            weighted(E // 2 - 2, 1)
            for p in range(2):
                weighted(E // 2 - 1, p)


_INS = ['x', 'L0_tok_w1', 'L0_tok_b1', 'L0_tok_w2', 'L0_tok_b2', 'L0_attn_W_qkv', 'L0_attn_W_out', 'L0_attn_b_out',
        'L0_ffn_Wr', 'L0_ffn_W1', 'L0_ffn_b1', 'L0_ffn_W2', 'L0_ffn_b2']
_OUT = ((16, 256, 128), 'float32')


def spectrum_bases(patch=200):
    k, n = np.arange(patch // 2 + 1), np.arange(patch // 2 + 1)
    angle = 2.0 * np.pi * ((n[:, None] * k[None, :]) % patch) / patch
    cosines, sines = np.cos(angle), -np.sin(angle)
    sines[:, 0] = 0.0
    sines[:, -1] = 0.0
    return cosines.astype(np.float32), sines[1:-1].astype(np.float32)


def build(nc, shapes):
    args = [nc.dram_tensor(f"in_{n}_dram", shape, dt, kind="ExternalInput").ap() for n, shape, dt in shapes]
    cosines, sines = spectrum_bases()
    cos_c = nc.dram_tensor("cosines", cosines.shape, mybir.dt.float32, kind="ExternalInput").ap()
    sin_c = nc.dram_tensor("sines", sines.shape, mybir.dt.float32, kind="ExternalInput").ap()
    out = nc.dram_tensor("out_0_dram", _OUT[0], mybir.dt.float32, kind="ExternalOutput").ap()
    audio_tower(nc, *args, cos_c, sin_c, out)


def kernel(**inputs):
    import numpy as _np
    import concourse.bacc as _bacc
    from concourse import mybir as _mybir
    from concourse.bass_utils import run_bass_kernel_spmd as _run

    nc = _bacc.Bacc("TRN2", target_bir_lowering=False, num_devices=1)
    cosines, sines = spectrum_bases()
    arrays, shapes = {"cosines": cosines, "sines": sines}, []
    for name in _INS:
        a = _np.ascontiguousarray(inputs[name])
        arrays[f"in_{name}_dram"] = a
        shapes.append((name, a.shape, _mybir.dt.from_np(a.dtype)))
    build(nc, shapes)
    r = _run(nc, [arrays], core_ids=[0])
    return r.results[0]["out_0_dram"]
```
